# Optimizing a Trainium2 kernel written in Bass

```python
import numpy as np
import jax
import jax.numpy as jnp

def _softmax(x, axis=-1):
    return jax.nn.softmax(x, axis=axis)

def _gelu(x):
    return jax.nn.gelu(x, approximate=True)

def _silu(x):
    return jax.nn.silu(x)

def _sigmoid(x):
    return jax.nn.sigmoid(x)

def _layernorm(x, axis=-1, eps=1e-05):
    m = jnp.mean(x, axis=axis, keepdims=True)
    v = jnp.var(x, axis=axis, keepdims=True)
    return (x - m) / jnp.sqrt(v + eps)

def _scatter_add(tgt, idx, src, axis=0):
    return tgt.at[idx].add(src)

def _segment_sum(src, seg, n):
    return jax.ops.segment_sum(src, seg, n)
kernel_name = 'mk_gnn_preln_d4_gnn_r8_da973c'

def setup_inputs(seed: int=0):
    np.random.seed(seed)
    _w = jnp.asarray

    def _rec_inputs():
        import jax
        import jax.numpy as jnp
        _gk = jax.random.key(seed)
        x = -0.0005121 + 1.001 * jax.random.normal(jax.random.fold_in(_gk, 1), (6250, 64), jnp.float32)
        src = jax.random.randint(jax.random.fold_in(_gk, 2), (200000,), 0, 6250, jnp.int32)
        dst = jnp.minimum((6250 * jax.random.uniform(jax.random.fold_in(_gk, 3), (200000,)) ** 2.0).astype(jnp.int32), 49999)
        _o = jnp.argsort(dst, stable=True)
        src = src[_o]
        dst = dst[_o]
        edge_attr_32 = -5.3897e-05 + 0.999841 * jax.random.normal(jax.random.fold_in(_gk, 12), (200000, 32), jnp.float32)
        edge_type_8 = jax.random.randint(jax.random.fold_in(_gk, 14), (200000,), 0, 8, jnp.int32)
        edge_weight = 0.00121237 + 1.00026 * jax.random.normal(jax.random.fold_in(_gk, 15), (200000,), jnp.float32)
        edge_weight_n2 = 0.00121237 + 1.00026 * jax.random.normal(jax.random.fold_in(_gk, 16), (200000,), jnp.float32)
        return (x, src, dst, edge_attr_32, edge_type_8, edge_weight, edge_weight_n2)
    x, src, dst, edge_attr_32, edge_type_8, edge_weight, edge_weight_n2 = _rec_inputs()

    def _L0_gnn_setup():
        import jax, jax.numpy as jnp
        import numpy as np
        N_NODES = 6250
        N_EDGES = 100000
        NODE_DIM = 64
        EDGE_DIM = 32
        OUT_FEATS = 64
        key = jax.random.key(seed)
        k1, k2, k3, k4, k5, k6 = jax.random.split(key, 6)
        node_features = jax.random.normal(k1, (N_NODES, NODE_DIM), dtype=jnp.float32)
        edge_features = jax.random.normal(k2, (N_EDGES, EDGE_DIM), dtype=jnp.float32)
        src = jax.random.randint(k3, (N_EDGES,), 0, N_NODES, dtype=jnp.int64 if jax.config.jax_enable_x64 else jnp.int32)
        dst = jax.random.randint(k4, (N_EDGES,), 0, N_NODES, dtype=jnp.int64 if jax.config.jax_enable_x64 else jnp.int32)
        in_dim = 2 * NODE_DIM + EDGE_DIM
        bound = 1.0 / np.sqrt(in_dim)
        W = jax.random.uniform(k5, (OUT_FEATS, in_dim), minval=-bound, maxval=bound, dtype=jnp.float32)
        b = jax.random.uniform(k6, (OUT_FEATS,), minval=-bound, maxval=bound, dtype=jnp.float32)
        return {'node_features': node_features, 'edge_features': edge_features, 'src': src, 'dst': dst, 'W': W, 'b': b}
    _L0_gnn_all = _L0_gnn_setup()
    _L0_gnn_in = {k: v for k, v in _L0_gnn_all.items() if k in ('W', 'b')}
    del _L0_gnn_all

    def _L1_gnn_setup():
        import jax, jax.numpy as jnp
        import numpy as np
        V, E = (6250, 100000)
        D_NODE, D_EDGE, D_OUT = (64, 32, 64)
        SLOPE = 0.2
        key = jax.random.key(seed)
        ks = jax.random.split(key, 12)
        inp = {'node_feats': jax.random.normal(ks[0], (V, D_NODE), dtype=jnp.float32), 'edge_feats': jax.random.normal(ks[1], (E, D_EDGE), dtype=jnp.float32), 'edge_index': jax.random.randint(ks[2], (2, E), 0, V, dtype=jnp.int64), 'W_q': jax.random.normal(ks[3], (D_NODE, D_OUT), dtype=jnp.float32) / np.sqrt(D_NODE), 'b_q': jax.random.normal(ks[4], (D_OUT,), dtype=jnp.float32) * 0.02, 'W_k': jax.random.normal(ks[5], (D_NODE, D_OUT), dtype=jnp.float32) / np.sqrt(D_NODE), 'b_k': jax.random.normal(ks[6], (D_OUT,), dtype=jnp.float32) * 0.02, 'W_v': jax.random.normal(ks[7], (D_NODE, D_OUT), dtype=jnp.float32) / np.sqrt(D_NODE), 'b_v': jax.random.normal(ks[8], (D_OUT,), dtype=jnp.float32) * 0.02, 'W_e': jax.random.normal(ks[9], (D_EDGE, D_OUT), dtype=jnp.float32) / np.sqrt(D_EDGE), 'b_e': jax.random.normal(ks[10], (D_OUT,), dtype=jnp.float32) * 0.02, 'a_w': jax.random.normal(ks[11], (D_OUT, 1), dtype=jnp.float32) / np.sqrt(D_OUT), 'a_b': jnp.zeros((1,), dtype=jnp.float32)}
        return inp
    _L1_gnn_all = _L1_gnn_setup()
    _L1_gnn_in = {k: v for k, v in _L1_gnn_all.items() if k in ('W_q', 'b_q', 'W_k', 'b_k', 'W_v', 'b_v', 'W_e', 'b_e', 'a_w', 'a_b')}
    del _L1_gnn_all

    def _L2_gnn_setup():
        import jax, jax.numpy as jnp
        import numpy as np
        N_NODES = 12500
        N_EDGES = 200000
        D_FEAT = 64
        key = jax.random.key(seed)
        k1, k2, k3, k4 = jax.random.split(key, 4)
        inputs = jax.random.normal(k1, (N_NODES, D_FEAT), dtype=jnp.float32)
        eidx = jax.random.randint(k2, (2, N_EDGES), 0, N_NODES, dtype=jnp.int32)
        enorm = jax.random.uniform(k3, (N_EDGES,), dtype=jnp.float32)
        esgn = jax.random.normal(k4, (N_EDGES,), dtype=jnp.float32)
        return {'inputs': inputs, 'eidx': eidx, 'enorm': enorm, 'esgn': esgn}
    _L2_gnn_all = _L2_gnn_setup()
    _L2_gnn_in = {k: v for k, v in _L2_gnn_all.items() if k in ()}
    del _L2_gnn_all

    def _L3_gnn_setup():
        import jax, jax.numpy as jnp
        import numpy as np
        N_NODES = 6250
        N_EDGES = 100000
        IN_DIM = 64
        OUT_DIM = 64
        N_REL = 8
        N_RULES = 32
        N_ACTIVE = 4
        LN_EPS = 1e-05

        def _seg_softmax(scores, seg, num_segments):
            m = jax.ops.segment_max(scores, seg, num_segments=num_segments)
            e = jnp.exp(scores - m[seg])
            d = jax.ops.segment_sum(e, seg, num_segments=num_segments)
            return e / d[seg]
        key = jax.random.key(seed)
        ks = jax.random.split(key, 12)
        x = jax.random.normal(ks[0], (N_NODES, IN_DIM), dtype=jnp.float32)
        edge_index = jax.random.randint(ks[1], (2, N_EDGES), 0, N_NODES, dtype=jnp.int64)
        edge_type = jax.random.randint(ks[2], (N_EDGES,), 0, N_REL, dtype=jnp.int64)
        rule_ids = jax.random.randint(ks[3], (N_ACTIVE,), 0, N_RULES, dtype=jnp.int64)
        W_r = jax.random.normal(ks[4], (N_REL, IN_DIM, OUT_DIM), dtype=jnp.float32) * (2.0 / (IN_DIM + OUT_DIM)) ** 0.5
        Wq_w = jax.random.normal(ks[5], (IN_DIM, OUT_DIM), dtype=jnp.float32) * (1.0 / IN_DIM) ** 0.5
        Wq_bias = jnp.zeros((OUT_DIM,), dtype=jnp.float32)
        Wk_w = jax.random.normal(ks[6], (3 * IN_DIM, OUT_DIM), dtype=jnp.float32) * (1.0 / (3 * IN_DIM)) ** 0.5
        Wk_bias = jnp.zeros((OUT_DIM,), dtype=jnp.float32)
        rule_emb = jax.random.normal(ks[7], (N_RULES, IN_DIM), dtype=jnp.float32) * (2.0 / (N_RULES + IN_DIM)) ** 0.5
        bias = jnp.zeros((OUT_DIM,), dtype=jnp.float32)
        ln_g = jnp.ones((OUT_DIM,), dtype=jnp.float32)
        ln_b = jnp.zeros((OUT_DIM,), dtype=jnp.float32)
        return {'x': x, 'edge_index': edge_index, 'edge_type': edge_type, 'rule_ids': rule_ids, 'W_r': W_r, 'Wq_w': Wq_w, 'Wq_bias': Wq_bias, 'Wk_w': Wk_w, 'Wk_bias': Wk_bias, 'rule_emb': rule_emb, 'bias': bias, 'ln_g': ln_g, 'ln_b': ln_b}
    _L3_gnn_all = _L3_gnn_setup()
    _L3_gnn_in = {k: v for k, v in _L3_gnn_all.items() if k in ('rule_ids', 'W_r', 'Wq_w', 'Wq_bias', 'Wk_w', 'Wk_bias', 'rule_emb', 'bias', 'ln_g', 'ln_b')}
    del _L3_gnn_all
    return {'x': x, 'src': src, 'dst': dst, 'edge_attr_32': edge_attr_32, 'edge_type_8': edge_type_8, 'edge_weight': edge_weight, 'edge_weight_n2': edge_weight_n2, 'L0_gnn_W': _L0_gnn_in['W'], 'L0_gnn_b': _L0_gnn_in['b'], 'L1_gnn_W_q': _L1_gnn_in['W_q'], 'L1_gnn_b_q': _L1_gnn_in['b_q'], 'L1_gnn_W_k': _L1_gnn_in['W_k'], 'L1_gnn_b_k': _L1_gnn_in['b_k'], 'L1_gnn_W_v': _L1_gnn_in['W_v'], 'L1_gnn_b_v': _L1_gnn_in['b_v'], 'L1_gnn_W_e': _L1_gnn_in['W_e'], 'L1_gnn_b_e': _L1_gnn_in['b_e'], 'L1_gnn_a_w': _L1_gnn_in['a_w'], 'L1_gnn_a_b': _L1_gnn_in['a_b'], 'L3_gnn_rule_ids': _L3_gnn_in['rule_ids'], 'L3_gnn_W_r': _L3_gnn_in['W_r'], 'L3_gnn_Wq_w': _L3_gnn_in['Wq_w'], 'L3_gnn_Wq_bias': _L3_gnn_in['Wq_bias'], 'L3_gnn_Wk_w': _L3_gnn_in['Wk_w'], 'L3_gnn_Wk_bias': _L3_gnn_in['Wk_bias'], 'L3_gnn_rule_emb': _L3_gnn_in['rule_emb'], 'L3_gnn_bias': _L3_gnn_in['bias'], 'L3_gnn_ln_g': _L3_gnn_in['ln_g'], 'L3_gnn_ln_b': _L3_gnn_in['ln_b']}

def reference(x, src, dst, edge_attr_32, edge_type_8, edge_weight, edge_weight_n2, L0_gnn_W, L0_gnn_b, L1_gnn_W_q, L1_gnn_b_q, L1_gnn_W_k, L1_gnn_b_k, L1_gnn_W_v, L1_gnn_b_v, L1_gnn_W_e, L1_gnn_b_e, L1_gnn_a_w, L1_gnn_a_b, L3_gnn_rule_ids, L3_gnn_W_r, L3_gnn_Wq_w, L3_gnn_Wq_bias, L3_gnn_Wk_w, L3_gnn_Wk_bias, L3_gnn_rule_emb, L3_gnn_bias, L3_gnn_ln_g, L3_gnn_ln_b):
    import jax
    import jax.numpy as jnp

    def _L0_gnn_ref(node_features, edge_features, src, dst, W, b):
        import jax, jax.numpy as jnp
        import numpy as np
        N_NODES = 6250
        N_EDGES = 100000
        NODE_DIM = 64
        EDGE_DIM = 32
        OUT_FEATS = 64
        msg = jnp.concatenate([node_features[src], edge_features], axis=1)
        agg = jax.ops.segment_sum(msg, dst, num_segments=node_features.shape[0])
        h = jnp.concatenate([node_features, agg], axis=1)
        h = h @ W.T + b
        return jax.nn.relu(h)

    def _L1_gnn_ref(node_feats, edge_feats, edge_index, W_q, b_q, W_k, b_k, W_v, b_v, W_e, b_e, a_w, a_b):
        import jax, jax.numpy as jnp
        import numpy as np
        V, E = (6250, 100000)
        D_NODE, D_EDGE, D_OUT = (64, 32, 64)
        SLOPE = 0.2
        src, dest = (edge_index[0], edge_index[1])
        n_nodes = node_feats.shape[0]
        Q = node_feats[src] @ W_q + b_q
        K = node_feats[dest] @ W_k + b_k
        Vv = node_feats[dest] @ W_v + b_v
        bias = edge_feats @ W_e + b_e
        pre = Q + K + bias
        act = jnp.where(pre >= 0, pre, SLOPE * pre)
        scores = act @ a_w + a_b
        seg_max = jax.ops.segment_max(scores, dest, num_segments=n_nodes)
        ex = jnp.exp(scores - seg_max[dest])
        denom = jax.ops.segment_sum(ex, dest, num_segments=n_nodes)
        alpha = ex / denom[dest]
        node_hiddens = jax.ops.segment_sum(alpha * Vv, dest, num_segments=n_nodes)
        return node_hiddens

    def _L2_gnn_ref(inputs, eidx, enorm, esgn):
        import jax, jax.numpy as jnp
        import numpy as np
        N_NODES = 12500
        N_EDGES = 200000
        D_FEAT = 64
        sidx, tidx = (eidx[0], eidx[1])
        message = inputs[sidx] * (esgn * enorm)[:, None]
        res = jax.ops.segment_sum(message, tidx, num_segments=inputs.shape[0])
        return res

    def _L3_gnn_ref(x, edge_index, edge_type, rule_ids, W_r, Wq_w, Wq_bias, Wk_w, Wk_bias, rule_emb, bias, ln_g, ln_b):
        import jax, jax.numpy as jnp
        import numpy as np
        N_NODES = 6250
        N_EDGES = 100000
        IN_DIM = 64
        OUT_DIM = 64
        N_REL = 8
        N_RULES = 32
        N_ACTIVE = 4
        LN_EPS = 1e-05

        def _seg_softmax(scores, seg, num_segments):
            m = jax.ops.segment_max(scores, seg, num_segments=num_segments)
            e = jnp.exp(scores - m[seg])
            d = jax.ops.segment_sum(e, seg, num_segments=num_segments)
            return e / d[seg]
        src, dst = (edge_index[0], edge_index[1])
        num_nodes, in_dim = x.shape
        num_rel, _, out_dim = W_r.shape
        x_src = x[src]
        q = x[dst] @ Wq_w + Wq_bias
        rel_emb = W_r.mean(axis=-1)[edge_type]
        Wk1, Wk2, Wk3 = (Wk_w[:in_dim], Wk_w[in_dim:2 * in_dim], Wk_w[2 * in_dim:])
        key_base = x_src @ Wk1 + rel_emb @ Wk2 + Wk_bias
        h_R = rule_emb[rule_ids]
        key_rule = h_R @ Wk3
        scale = 1.0 / out_dim ** 0.5
        score_base = jnp.einsum('eo,eo->e', q, key_base)
        score_rule = jnp.einsum('eo,ro->er', q, key_rule)
        scores = (score_base[:, None] + score_rule) * scale
        attn = jax.vmap(lambda s: _seg_softmax(s, dst, num_nodes), in_axes=1, out_axes=1)(scores)
        mean_attn = attn.mean(axis=1)
        msg = jnp.zeros((x_src.shape[0], out_dim), dtype=x.dtype)
        for r in range(num_rel):
            msg = jnp.where((edge_type == r)[:, None], x_src @ W_r[r], msg)
        out = jax.ops.segment_sum(msg * mean_attn[:, None], dst, num_segments=num_nodes)
        out = out + bias
        mu = out.mean(axis=-1, keepdims=True)
        var = ((out - mu) ** 2).mean(axis=-1, keepdims=True)
        out = (out - mu) * jax.lax.rsqrt(var + LN_EPS) * ln_g + ln_b
        return jax.nn.relu(out)
    edge_index = jnp.stack([src, dst])
    h = jnp.maximum(_layernorm(x, axis=-1), 0.0)
    x = x + _L0_gnn_ref(h, edge_attr_32, src, dst, L0_gnn_W, L0_gnn_b)
    h = jnp.maximum(_layernorm(x, axis=-1), 0.0)
    x = x + _L1_gnn_ref(h, edge_attr_32, edge_index, L1_gnn_W_q, L1_gnn_b_q, L1_gnn_W_k, L1_gnn_b_k, L1_gnn_W_v, L1_gnn_b_v, L1_gnn_W_e, L1_gnn_b_e, L1_gnn_a_w, L1_gnn_a_b)
    h = jnp.maximum(_layernorm(x, axis=-1), 0.0)
    x = x + _L2_gnn_ref(h, edge_index, edge_weight, edge_weight_n2)
    h = jnp.maximum(_layernorm(x, axis=-1), 0.0)
    x = x + _L3_gnn_ref(h, edge_index, edge_type_8, L3_gnn_rule_ids, L3_gnn_W_r, L3_gnn_Wq_w, L3_gnn_Wq_bias, L3_gnn_Wk_w, L3_gnn_Wk_bias, L3_gnn_rule_emb, L3_gnn_bias, L3_gnn_ln_g, L3_gnn_ln_b)
    return x

_drawn_inputs = setup_inputs


def setup_inputs(seed=0):
    import zlib

    import numpy as np

    out = dict(_drawn_inputs(seed))
    spreads = {'L3_gnn_Wq_bias': (0.0, 0.8),
     'L3_gnn_Wk_bias': (0.0, 2.0),
     'L3_gnn_bias': (0.0, 0.381),
     'L3_gnn_ln_g': (1.0, 0.6),
     'L3_gnn_ln_b': (0.0, 0.8)}
    factors = {'L0_gnn_b': 5.336,
     'L1_gnn_W_q': 64.0,
     'L1_gnn_b_q': 64.0,
     'L1_gnn_W_k': 64.0,
     'L1_gnn_b_k': 64.0,
     'L1_gnn_b_v': 8.0,
     'L1_gnn_W_e': 64.0,
     'L1_gnn_b_e': 64.0,
     'L1_gnn_a_w': 64.0,
     'L3_gnn_Wq_w': 4.705,
     'L3_gnn_Wk_w': 4.735,
     'L3_gnn_rule_emb': 64.0}
    for name, (base, spread) in spreads.items():
        noise = np.random.default_rng([zlib.crc32(name.encode()), seed]).standard_normal(out[name].shape)
        drawn = base * np.exp(spread * noise) if base else spread * noise
        out[name] = jnp.asarray(drawn.astype(out[name].dtype))
    for name, factor in factors.items():
        out[name] = (out[name] * factor).astype(out[name].dtype)
    return out
```

```python
import contextlib

import numpy as np

import concourse.bass as bass
from concourse import mybir

F32 = mybir.dt.float32
I32 = mybir.dt.int32
ALU = mybir.AluOpType
ACT = mybir.ActivationFunctionType
AX = mybir.AxisListType.X

P = 128
N_NODES, N_EDGES, D, D_EDGE = 6250, 200000, 64, 32
N_REL, N_ACTIVE = 8, 4
LN_EPS = 1e-5
SLOPE = 0.2
ATT_SCALE = 1.0 / D ** 0.5
FAR_BELOW = -1.0e30
TINY = 1.0e-30

TILES_PER_BATCH = 4
BATCH = TILES_PER_BATCH * P
UNROLL = 8
N_BATCHES = -(-N_EDGES // (BATCH * UNROLL)) * UNROLL
N_TILES = N_BATCHES * TILES_PER_BATCH
E_PAD = N_BATCHES * BATCH
BATCH_ROWS = N_BATCHES // 4

NODE_TILES = -(-(N_NODES + 1) // P) + 1
N_PAD = NODE_TILES * P
WINDOW, WINDOW_STEP = 128, 32
LAST_BASE = N_PAD - WINDOW
N_CHUNKS = LAST_BASE // WINDOW_STEP + 1
RING = 4
BANK = 512


class Batch:

    def __init__(self, i, off):
        self.i, self.off = i, off
        self.v = off if i is None else i * UNROLL + off

    def slot(self, ring):
        return self.off % ring

    def uses(self, ring):
        return self.off // ring if self.i is None else self.i * (UNROLL // ring) + self.off // ring

    def early(self, ring):
        return self.i is None and self.off < ring


def done(eng, sem, b):
    eng.wait_ge(sem, b.v + 1)


def free(eng, sem, b, ring):
    if not b.early(ring):
        eng.wait_ge(sem, b.v + (1 - ring))


def landed(eng, sems, b, per_use):
    eng.wait_ge(sems[b.slot(RING)], (b.uses(RING) + 1) * per_use)


def pipeline(eng, stages):
    def step(i, t):
        for lag, stage in stages:
            b = t - lag
            if i is not None or 0 <= b < N_BATCHES:
                stage(Batch(i, b))
    for t in range(UNROLL):
        step(None, t)
    with eng.Fori(1, N_BATCHES // UNROLL) as i:
        for u in range(UNROLL):
            step(i, u)
    for t in range(N_BATCHES, N_BATCHES + max(lag for lag, _ in stages)):
        step(None, t)


class Phase:

    def __init__(self, nc, name):
        self.nc, self.name, self.sems, self.shared = nc, name, [], []
        self.stack = contextlib.ExitStack()

    def sem(self, what):
        s = self.stack.enter_context(self.nc.semaphore(f"{self.name}_{what}"))
        self.sems.append(s)
        return s

    def use(self, sems):
        self.shared = sems
        return sems

    def __enter__(self):
        self.block_stack = contextlib.ExitStack()
        return self

    def open(self):
        return self.block_stack.enter_context(self.nc.Block())

    def __exit__(self, *error):
        self.block_stack.__exit__(*error)
        if error[0] is None:
            nums = [s.num for s in self.sems]
            self.nc.all_engine_barrier(sems_to_clear=range(min(nums), max(nums) + 1))
            if self.shared:
                nums = [s.num for s in self.shared]
                self.nc.all_engine_barrier(sems_to_clear=range(min(nums), max(nums) + 1))
        self.stack.__exit__(*error)
        return False


class Chain:

    def __init__(self, eng, sem):
        self.eng, self.sem, self.n = eng, sem, 0

    def do(self, ins):
        self.n += 1
        ins.then_inc(self.sem, 1)
        self.eng.wait_ge(self.sem, self.n)


def graph_layers(nc, a, out):
    ctx = contextlib.ExitStack()
    with ctx:
        def sb(name, shape, dt=F32):
            return ctx.enter_context(nc.sbuf_tensor(name, shape, dt))

        node_rows = nc.dram_tensor("node_rows", (N_PAD, D), F32).ap()
        rel_rows = nc.dram_tensor("rel_rows", (N_PAD * N_REL, 2 * D), F32).ap()
        spill = nc.dram_tensor("spill", (N_BATCHES, P, TILES_PER_BATCH * D), F32).ap()
        batch_facts = nc.dram_tensor("batch_facts", (2, N_BATCHES), I32).ap()

        ident = sb("ident", [P, P])
        iota = sb("iota", [P, P])
        one = sb("one", [1, 1])

        src_idx = sb("src_idx", [P, N_TILES], I32)
        rel_idx = sb("rel_idx", [P, N_TILES], I32)
        dst_rel0 = sb("dst_rel0", [P, N_TILES])
        dst_rel = sb("dst_rel", [P, N_TILES])
        weight = sb("weight", [P, N_TILES])
        score = sb("score", [P, N_TILES])
        in_window = sb("in_window", [P, N_TILES])

        base0 = sb("base0", [1, N_BATCHES], I32)
        base = sb("base", [1, N_BATCHES], I32)
        n_windows = sb("n_windows", [1, 1], I32)

        x = sb("x", [P, NODE_TILES, D])
        featT = sb("featT", [P, N_PAD])
        accT = sb("accT", [P, N_PAD])
        by_chunk = sb("by_chunk", [P, N_CHUNKS * D])
        small_by_chunk = sb("small_by_chunk", [P, N_CHUNKS * N_ACTIVE])
        node_a = sb("node_a", [P, NODE_TILES])
        node_b = sb("node_b", [P, NODE_TILES])
        centred = by_chunk[:, 0:NODE_TILES * D].rearrange("p (j d) -> p j d", d=D)
        normed = by_chunk[:, NODE_TILES * D:2 * NODE_TILES * D].rearrange("p (j d) -> p j d", d=D)

        idx_slots = sb("idx_slots", [P, 2, RING * TILES_PER_BATCH], I32)
        rows = sb("rows", [P, RING, TILES_PER_BATCH, 2 * D])
        onehot = sb("onehot", [P, RING, TILES_PER_BATCH, P])
        onehotT = sb("onehotT", [P, 2, TILES_PER_BATCH, P])
        penalty = sb("penalty", [P, 2, TILES_PER_BATCH, P])
        masked = sb("masked", [P, 2, TILES_PER_BATCH, P])
        edge_in = sb("edge_in", [P, RING, BANK])
        spill_out = edge_in[:, :, 0:TILES_PER_BATCH * D]
        pre = sb("pre", [P, 2, TILES_PER_BATCH, D])
        small_a = sb("small_a", [P, 2, TILES_PER_BATCH])
        small_b = sb("small_b", [P, 2, TILES_PER_BATCH])
        batch_max = sb("batch_max", [P, 2])
        ex_in = sb("ex_in", [P, 2, TILES_PER_BATCH * N_ACTIVE])
        ex = sb("ex", [P, RING, TILES_PER_BATCH * N_ACTIVE])

        w0_self = sb("w0_self", [D + 1, D])
        w0_agg = sb("w0_agg", [D + D_EDGE, D])
        w1_q = sb("w1_q", [D + 3, D])
        w1_k = sb("w1_k", [D, D])
        w1_v = sb("w1_v", [D + 1, D])
        w1_e = sb("w1_e", [D_EDGE, D])
        a_w = sb("a_w", [P, D])
        a_b = sb("a_b", [P, 1])
        w3_rel = sb("w3_rel", [D, N_REL, D])
        w3_q = sb("w3_q", [D + 1, D])
        w3_qT = sb("w3_qT", [D, D + 1])
        w3_k = sb("w3_k", [D, 3, D])
        w3_table = penalty[0:D + 2, :, :, :].rearrange("p s g n -> p (s g) n")
        rel_mean = sb("rel_mean", [D, N_REL])
        rule_ids = sb("rule_ids", [N_ACTIVE, 1], I32)
        rules = sb("rules", [N_ACTIVE, D])
        rulesT = sb("rulesT", [D, N_ACTIVE])
        rule_keyT = sb("rule_keyT", [D, N_ACTIVE])
        w3_rule = sb("w3_rule", [D + 1, N_ACTIVE])
        bias3 = sb("bias3", [P, 3, D])

        gather_sems = [ctx.enter_context(nc.semaphore(f"gathered{n}")) for n in range(RING)]
        s_rules = ctx.enter_context(nc.semaphore("gathered_rules"))

        banks = [ctx.enter_context(nc.psum_tensor(f"bank{n}", [P, BANK], F32)) for n in range(8)]

        dst_rows = accT[0:BATCH_ROWS, 0:4 * BATCH].bitcast(I32)
        dst_rows_f = featT[0:BATCH_ROWS, 0:4 * BATCH]
        dst_raw = rel_idx
        fact_i = idx_slots[0:BATCH_ROWS, 0, :]
        base_wide = penalty[:, 0, :, :].rearrange("p g n -> p (g n)")[:, 0:N_BATCHES].bitcast(I32)
        base_wide_f = masked[:, 0, :, :].rearrange("p g n -> p (g n)")[:, 0:N_BATCHES]
        with Phase(nc, "load") as ph:
            s_dst, s_in, s_w, s_const = (ph.sem(n) for n in ("dst", "edges", "weights", "consts"))
            s_chain, s_fact, s_back, s_rule = (
                ph.sem(n) for n in ("chain", "fact", "back", "rule"))
            block = ph.open()
            edge_loads = [(dst_raw[:, :], a["dst_l"]), (src_idx[:, :], a["src_l"]),
                          (score[:, :], a["w2_l"]), (weight[:, :], a["w_l"]),
                          (in_window[:, :].bitcast(I32), a["type_l"]),
                          (x[:, :, :].rearrange("p j d -> p (j d)"), a["x_l"])]
            weight_loads = [(w0_self, a["w0_self"]), (w0_agg, a["w0_agg"]), (w1_q, a["w1_q"]),
                            (w1_k, a["w1_k"]), (w1_v, a["w1_v"]), (w1_e, a["w1_e"]),
                            (w3_q, a["w3_q"]), (w3_qT, a["w3_qT"]),
                            (w3_rel, a["w3_rel"].rearrange("i (r o) -> i r o", o=D)),
                            (w3_k, a["w3_k"].rearrange("i (r o) -> i r o", o=D))]

            @block.sync
            def _(sp):
                sp.dma_start(dst_rows, a["dst_b"]).then_inc(s_dst, 16)
                for to, of in edge_loads:
                    sp.dma_start(to, of).then_inc(s_in, 16)
                sp.wait_ge(s_fact, 1)
                sp.dma_start(batch_facts.rearrange("f (p q) -> p f q", q=4),
                             fact_i[:, 0:8].rearrange("p (f q) -> p f q", q=4)).then_inc(s_back, 16)
                sp.wait_ge(s_back, 16)
                sp.dma_start(base0[:, :], batch_facts[0:1, :]).then_inc(s_back, 16)
                sp.dma_start(base[:, :], batch_facts[1:2, :]).then_inc(s_back, 16)
                sp.dma_start(base_wide, batch_facts[0:1, :].to_broadcast([P, N_BATCHES]))\
                  .then_inc(s_back, 16)

            @block.scalar
            def _(act):
                for to, of in weight_loads:
                    act.dma_start(to[:], of).then_inc(s_w, 16)
                act.dma_start(a_w[:, :], a["a_w"].to_broadcast([P, D])).then_inc(s_w, 16)
                act.dma_start(a_b[:, :], a["a_b"].to_broadcast([P, 1])).then_inc(s_w, 16)
                act.dma_start(bias3[:, :, :].rearrange("p r o -> p (r o)"),
                              a["bias3"].to_broadcast([P, 3 * D])).then_inc(s_w, 16)
                act.dma_start(rule_ids[:, :], a["rule_ids"]).then_inc(s_rule, 16)
                act.wait_ge(s_w, 16 * (len(weight_loads) + 3))

            @block.gpsimd
            def _(pool):
                pool.memset(ident[:, :], 0.0).then_inc(s_const, 1)
                pool.iota(iota[:, :], [[1, P]], base=0, channel_multiplier=0,
                          allow_small_or_imprecise_dtypes=True).then_inc(s_const, 1)
                pool.memset(one[:, :], 1.0).then_inc(s_const, 1)
                pool.wait_ge(s_const, 3)
                pool.affine_select(out=ident[:, :], in_=ident[:, :], compare_op=ALU.not_equal,
                                   fill=1.0, base=0, pattern=[[-1, P]], channel_multiplier=1)\
                    .then_inc(s_const, 1)
                pool.wait_ge(s_rule, 16)
                pool.indirect_dma_start(
                    out=rules[:, :], out_offset=None, in_=a["rule_emb"],
                    in_offset=bass.IndirectOffsetOnAxis(ap=rule_ids[:, 0:1], axis=0))\
                    .then_inc(s_rules, 16)
                pool.wait_ge(s_rules, 16)

            @block.vector
            def _(dve):
                c = Chain(dve, s_chain)
                least, most = node_a[0:BATCH_ROWS, 0:4], node_a[0:BATCH_ROWS, 4:8]
                dve.wait_ge(s_dst, 16)
                rows4 = dst_rows_f.rearrange("p (q e) -> p q e", q=4)
                c.do(dve.tensor_copy(dst_rows_f, dst_rows))
                c.do(dve.tensor_reduce(least, rows4, AX, ALU.min))
                c.do(dve.tensor_reduce(most, rows4, AX, ALU.max))
                c.do(dve.tensor_copy(fact_i[:, 0:4], least))
                c.do(dve.tensor_copy(fact_i[:, 4:8], most))
                c.do(dve.tensor_single_scalar(fact_i[:, 0:4], fact_i[:, 0:4],
                                              WINDOW_STEP.bit_length() - 1,
                                              ALU.arith_shift_right))
                c.do(dve.tensor_single_scalar(fact_i[:, 0:4], fact_i[:, 0:4], WINDOW_STEP, ALU.mult))
                c.do(dve.tensor_tensor(fact_i[:, 4:8], fact_i[:, 4:8], fact_i[:, 0:4], ALU.subtract))
                dve.tensor_single_scalar(fact_i[:, 4:8], fact_i[:, 4:8], WINDOW.bit_length() - 1,
                                         ALU.arith_shift_right).then_inc(s_fact, 1)
                dve.memset(featT[64:96, :], 1.0).then_inc(s_fact, 1)
                dve.wait_ge(s_back, 64)
                c.do(dve.tensor_reduce(n_windows[:, :], base[:, :], AX, ALU.max))
                c.do(dve.tensor_single_scalar(n_windows[:, :], n_windows[:, :], 1, ALU.add))
                c.do(dve.tensor_copy(base_wide_f, base_wide))
                dve.wait_ge(s_in, 16 * len(edge_loads))
                c.do(dve.tensor_copy(dst_rel0[:, :], dst_raw[:, :]))
                by_batch = dst_rel0[:, :].rearrange("p (b g) -> p b g", g=TILES_PER_BATCH)
                c.do(dve.tensor_tensor(by_batch, by_batch, base_wide_f.unsqueeze(2).to_broadcast(
                    [P, N_BATCHES, TILES_PER_BATCH]), ALU.subtract))
                c.do(dve.tensor_single_scalar(rel_idx[:, :], src_idx[:, :], N_REL, ALU.mult))
                c.do(dve.tensor_tensor(rel_idx[:, :], rel_idx[:, :],
                                       in_window[:, :].bitcast(I32), ALU.add))
                c.do(dve.tensor_tensor(weight[:, :], score[:, :], weight[:, :], ALU.mult))

        def layer_norm(name, rows_out=False):
            with Phase(nc, name) as ph:
                s_chain, s_var, s_std, s_h, s_t, s_ev, s_out = (
                    ph.sem(n) for n in ("chain", "var", "std", "normed", "turned", "copied", "out"))
                block = ph.open()
                groups = [(g, min(4, NODE_TILES - g)) for g in range(0, NODE_TILES, 4)]

                @block.vector
                def _(dve):
                    c = Chain(dve, s_chain)
                    wide = [P, NODE_TILES, D]
                    c.do(dve.reduce_sum(node_a[:, :], x[:, :, :], AX))
                    c.do(dve.tensor_single_scalar(node_a[:, :], node_a[:, :], 1.0 / D, ALU.mult))
                    c.do(dve.tensor_tensor(centred, x[:, :, :],
                                           node_a[:, :].unsqueeze(2).to_broadcast(wide), ALU.subtract))
                    c.do(dve.tensor_tensor(normed, centred, centred, ALU.mult))
                    c.do(dve.reduce_sum(node_a[:, :], normed, AX))
                    dve.tensor_scalar(node_a[:, :], node_a[:, :], 1.0 / D, LN_EPS, ALU.mult, ALU.add)\
                       .then_inc(s_var, 1)
                    dve.wait_ge(s_std, 1)
                    c.do(dve.reciprocal(node_b[:, :], node_b[:, :]))
                    dve.scalar_tensor_tensor(normed, centred, 0.0,
                                             node_b[:, :].unsqueeze(2).to_broadcast(wide),
                                             ALU.max, ALU.mult).then_inc(s_h, 1)

                @block.scalar
                def _(act):
                    act.wait_ge(s_var, 1)
                    act.activation(node_b[:, :], node_a[:, :], ACT.Sqrt).then_inc(s_std, 1)
                    for n, (g, k) in enumerate(groups):
                        act.wait_ge(s_t, n + 1)
                        act.activation(featT[0:D, g * P:(g + k) * P], banks[n % 4][0:D, 0:k * P],
                                       ACT.Copy).then_inc(s_ev, 1)

                @block.tensor
                def _(pe):
                    pe.wait_ge(s_h, 1)
                    for n, (g, k) in enumerate(groups):
                        if n >= 4:
                            pe.wait_ge(s_ev, n - 3)
                        for j in range(k):
                            last = pe.transpose(banks[n % 4][0:D, j * P:(j + 1) * P],
                                                normed[:, g + j, :], ident[:, :])
                        last.then_inc(s_t, 1)

                @block.sync
                def _(sp):
                    if rows_out:
                        sp.wait_ge(s_h, 1)
                        sp.dma_start(node_rows.rearrange("(j p) d -> p j d", p=P), normed)\
                          .then_inc(s_out, 16)
                        sp.wait_ge(s_out, 16)

        def products(name, n_items, per_bank, matmuls, take, stores=None):
            both = take.both
            with Phase(nc, name) as ph:
                s_pe, s_chain = ph.sem("filled"), ph.sem("chain")
                s_took = [ph.sem("took_dve"), ph.sem("took_act")]
                s_store = [ph.sem(f"store{n}") for n in range(RING)]
                block = ph.open()
                groups = [range(g, min(g + per_bank, n_items)) for g in range(0, n_items, per_bank)]
                who = [n % 2 if both else 0 for n in range(len(groups))]

                def taken(eng, n):
                    eng.wait_ge(s_took[who[n]], sum(w == who[n] for w in who[:n + 1]))

                @block.tensor
                def _(pe):
                    for n, items in enumerate(groups):
                        if n >= RING:
                            taken(pe, n - RING)
                        for place, item in enumerate(items):
                            last = matmuls(pe, item, banks[n % RING], place)
                        last.then_inc(s_pe, 1)

                def emptier(me):
                    def run(eng):
                        c = Chain(eng, s_chain) if me == 0 else None
                        for n, items in enumerate(groups):
                            if who[n] != me:
                                continue
                            eng.wait_ge(s_pe, n + 1)
                            if stores and n >= RING:
                                eng.wait_ge(s_store[n % RING], 16 * (n // RING))
                            if not both and n:
                                taken(eng, n - 1)
                            take(eng, c, n, items, banks[n % RING]).then_inc(s_took[me], 1)
                    return run
                block.vector(emptier(0))
                if both:
                    block.scalar(emptier(1))
                if stores:
                    @block.sync
                    def _(sp):
                        for n, items in enumerate(groups):
                            taken(sp, n)
                            stores(sp, n, items).then_inc(s_store[n % RING], 16)
                        for k in range(min(RING, len(groups))):
                            sp.wait_ge(s_store[k], 16 * len(range(k, len(groups), RING)))

        def copy(eng, to, of):
            if eng is nc.scalar:
                return eng.activation(to, of, ACT.Copy)
            return eng.tensor_copy(to, of)

        def table_by_chunk(name, w, k_rows):
            def matmuls(pe, c, bank, place):
                at = c * WINDOW_STEP
                return pe.matmul(bank[:, place * D:(place + 1) * D], featT[0:k_rows, at:at + P],
                                 w[:, :], start=True, stop=True)

            def take(eng, c, n, items, bank):
                return copy(eng, by_chunk[:, items[0] * D:(items[-1] + 1) * D],
                            bank[:, 0:len(items) * D])
            take.both = True
            products(name, N_CHUNKS, BANK // D, matmuls, take)

        def rows_view(items):
            return node_rows[items[0] * P:(items[-1] + 1) * P, :].rearrange("(j p) d -> p j d", p=P)

        def gather_stage(pool, indices, table, width, s_rows, s_idx, s_free):
            def gather(b):
                if b.slot(RING) == 0:
                    half = b.slot(2 * RING) // RING
                    pool.tensor_copy(idx_slots[:, half, :],
                                     indices[:, bass.ds(b.v * TILES_PER_BATCH,
                                                        RING * TILES_PER_BATCH)])\
                        .then_inc(s_idx, 1)
                    pool.wait_ge(s_idx, b.uses(RING) + 1)
                free(pool, s_free, b, RING)
                if b.i is not None:
                    pool.nop(nofuse=True)
                for g in range(TILES_PER_BATCH):
                    col = b.slot(RING) * TILES_PER_BATCH + g
                    half = b.slot(2 * RING) // RING
                    pool.indirect_dma_start(
                        out=rows[:, b.slot(RING), g, 0:width], out_offset=None, in_=table,
                        in_offset=bass.IndirectOffsetOnAxis(
                            ap=idx_slots[:, half, col:col + 1], axis=0))\
                        .then_inc(s_rows[b.slot(RING)], 16)
            return gather

        def end_gathers(pool):
            for s in gather_sems:
                pool.wait_ge(s, 16 * TILES_PER_BATCH * N_BATCHES // RING)
            pool.dma_reset(range(gather_sems[0].num, gather_sems[-1].num + 1))

        def tiles_of(t, b):
            return t[:, bass.ds(b.v * TILES_PER_BATCH, TILES_PER_BATCH)]

        def onehot_stage(dve, s_onehot, readers):
            def build(b):
                for s in readers:
                    free(dve, s, b, RING)
                wide = [P, TILES_PER_BATCH, P]
                dve.tensor_tensor(onehot[:, b.slot(RING), :, :],
                                  iota[:, :].unsqueeze(1).to_broadcast(wide),
                                  tiles_of(dst_rel, b).unsqueeze(2).to_broadcast(wide),
                                  ALU.is_equal).then_inc(s_onehot, 1)
            return build

        def read_base(eng, b):
            return eng.value_load(base[0:1, bass.ds(b.v, 1)], min_val=0, max_val=LAST_BASE)

        def turn_stage(pe, s_onehot, s_turned, s_copied):
            def turn(b):
                done(pe, s_onehot, b)
                free(pe, s_copied, b, 2)
                for g in range(TILES_PER_BATCH):
                    last = pe.transpose(banks[b.slot(2)][:, g * P:(g + 1) * P],
                                        onehot[:, b.slot(RING), g, :], ident[:, :])
                last.then_inc(s_turned, 1)
            return turn

        def copy_turned_stage(act, s_turned, s_copied, s_looked):
            def copy_turned(b):
                done(act, s_turned, b)
                free(act, s_looked, b, 2)
                act.activation(onehotT[:, b.slot(2), :, :].rearrange("p g e -> p (g e)"),
                               banks[b.slot(2)][:, :], ACT.Copy).then_inc(s_copied, 1)
            return copy_turned

        def window_loop(name, sweep, need_valid):
            with Phase(nc, name + "_first") as ph:
                s = ph.sem("set")
                block = ph.open()

                @block.vector
                def _(dve):
                    dve.tensor_copy(dst_rel[:, :], dst_rel0[:, :]).then_inc(s, 1)
                    dve.tensor_copy(base[:, :], base0[:, :]).then_inc(s, 1)
                    dve.wait_ge(s, 2)
            windows = nc.values_load(n_windows[0:1, 0:1], min_val=1, max_val=N_PAD // WINDOW + 1)
            with nc.Fori(0, windows):
                if need_valid:
                    with Phase(nc, name + "_valid") as ph:
                        s = ph.sem("set")
                        block = ph.open()

                        @block.vector
                        def _(dve):
                            c = Chain(dve, s)
                            c.do(dve.tensor_single_scalar(in_window[:, :], dst_rel[:, :], 0.0,
                                                          ALU.is_ge))
                            c.do(dve.scalar_tensor_tensor(in_window[:, :], dst_rel[:, :],
                                                          float(WINDOW), in_window[:, :],
                                                          ALU.is_lt, ALU.mult))
                sweep()
                with Phase(nc, name + "_next") as ph:
                    s = ph.sem("set")
                    block = ph.open()

                    @block.vector
                    def _(dve):
                        c = Chain(dve, s)
                        c.do(dve.tensor_single_scalar(dst_rel[:, :], dst_rel[:, :],
                                                      float(-WINDOW), ALU.add))
                        c.do(dve.tensor_scalar(base[:, :], base[:, :], WINDOW, LAST_BASE,
                                               ALU.add, ALU.min))

        def clear(name, *regions):
            with Phase(nc, name) as ph:
                s = ph.sem("set")
                block = ph.open()

                @block.vector
                def _(dve):
                    for r, value in regions:
                        dve.memset(r, value).then_inc(s, 1)
                    dve.wait_ge(s, len(regions))

        def sum_sweep(name, width, edge_rows, weighted):
            def sweep():
                with Phase(nc, name) as ph:
                    s_onehot, s_joined, s_sum, s_added, s_idx = (
                        ph.sem(n) for n in ("onehot", "joined", "summed", "added", "idx"))
                    s_rows = ph.use(gather_sems)
                    s_edge = [ph.sem(f"edge{n}") for n in range(RING)]
                    block = ph.open()
                    ew = TILES_PER_BATCH * D_EDGE

                    @block.gpsimd
                    def _(pool):
                        pipeline(pool, [(0, gather_stage(pool, src_idx, node_rows, D, s_rows, s_idx,
                                                         s_sum))])
                        end_gathers(pool)

                    if edge_rows:
                        @block.sync
                        def _(sp):
                            def stream(b):
                                free(sp, s_joined, b, RING)
                                sp.dma_start(edge_in[:, b.slot(RING), 0:ew],
                                             a["ea_l"][:, bass.ds(b.v * ew, ew)])\
                                  .then_inc(s_edge[b.slot(RING)], 16)
                            pipeline(sp, [(0, stream)])

                        @block.scalar
                        def _(act):
                            def join(b):
                                landed(act, s_edge, b, 16)
                                free(act, s_sum, b, RING)
                                act.activation(
                                    rows[:, b.slot(RING), :, D:D + D_EDGE],
                                    edge_in[:, b.slot(RING), 0:ew].rearrange(
                                        "p (g f) -> p g f", f=D_EDGE), ACT.Copy)\
                                    .then_inc(s_joined, 1)
                            pipeline(act, [(0, join)])

                    @block.tensor
                    def _(pe):
                        def sums(b):
                            done(pe, s_onehot, b)
                            landed(pe, s_rows, b, 16 * TILES_PER_BATCH)
                            if edge_rows:
                                done(pe, s_joined, b)
                            free(pe, s_added, b, 2)
                            for g in range(TILES_PER_BATCH):
                                last = pe.matmul(banks[b.slot(2)][0:width, 0:P],
                                                 rows[:, b.slot(RING), g, 0:width],
                                                 onehot[:, b.slot(RING), g, :],
                                                 start=(g == 0), stop=(g == TILES_PER_BATCH - 1))
                            last.then_inc(s_sum, 1)
                        pipeline(pe, [(0, sums)])

                    @block.vector
                    def _(dve):
                        def weighted_onehot(b):
                            free(dve, s_sum, b, RING)
                            for g in range(TILES_PER_BATCH):
                                col = bass.ds(b.v * TILES_PER_BATCH + g, 1)
                                last = dve.tensor_scalar(onehot[:, b.slot(RING), g, :], iota[:, :],
                                                         dst_rel[:, col], weight[:, col],
                                                         ALU.is_equal, ALU.mult)
                            last.then_inc(s_onehot, 1)

                        def add(b):
                            done(dve, s_sum, b)
                            at = accT[0:width, bass.ds(read_base(dve, b), WINDOW)]
                            if not b.early(1):
                                dve.wait_ge(s_added, b.v)
                            dve.tensor_tensor(at, banks[b.slot(2)][0:width, 0:P], at, ALU.add)\
                               .then_inc(s_added, 1)
                        build = (weighted_onehot if weighted else
                                 onehot_stage(dve, s_onehot, [s_sum]))
                        pipeline(dve, [(0, build), (2, add)])
            window_loop(name, sweep, False)

        def score_sweep(name, layer):
            width = D if layer == 1 else 2 * D

            def sweep():
                with Phase(nc, name) as ph:
                    (s_onehot, s_turned, s_copied, s_penalty, s_looked, s_pre, s_act, s_mul,
                     s_sum, s_valid, s_kept, s_masked, s_mturned, s_max, s_row, s_rowmax, s_idx,
                     s_packed) = (ph.sem(n) for n in (
                         "onehot", "turned", "copied", "penalty", "looked", "pre", "act", "mul",
                         "sum", "valid", "kept", "masked", "mturned", "max", "row", "rowmax",
                         "idx", "packed"))
                    s_rows = ph.use(gather_sems)
                    s_dma = [ph.sem(f"edge{n}") for n in range(RING)]
                    block = ph.open()
                    indices, table = (src_idx, node_rows) if layer == 1 else (rel_idx, rel_rows)
                    s_read = s_pre if layer == 1 else s_packed

                    @block.gpsimd
                    def _(pool):
                        pipeline(pool, [(0, gather_stage(pool, indices, table, width, s_rows,
                                                         s_idx, s_read))])
                        end_gathers(pool)

                    @block.sync
                    def _(sp):
                        def stream(b):
                            free(sp, s_looked, b, RING)
                            sp.dma_start(edge_in[0:D_EDGE, b.slot(RING), :],
                                         a["eaT_l"][:, bass.ds(b.v * BATCH, BATCH)])\
                              .then_inc(s_dma[b.slot(RING)], 16)

                        def store(b):
                            done(sp, s_packed, b)
                            sp.dma_start(spill[bass.ds(b.v, 1), :, :].rearrange("o p f -> (o p) f"),
                                         spill_out[:, b.slot(RING), :])\
                              .then_inc(s_dma[b.slot(RING)], 16)
                        pipeline(sp, [(0, stream if layer == 1 else store)])
                        if layer == 3:
                            for s in s_dma:
                                sp.wait_ge(s, 16 * N_BATCHES // RING)

                    @block.scalar
                    def _(act):
                        def penalties(b):
                            done(act, s_onehot, b)
                            free(act, s_masked, b, 2)
                            act.activation(penalty[:, b.slot(2), :, :],
                                           onehot[:, b.slot(RING), :, :], ACT.Copy,
                                           bias=FAR_BELOW, scale=-FAR_BELOW).then_inc(s_penalty, 1)

                        def pack(b):
                            landed(act, s_rows, b, 16 * TILES_PER_BATCH)
                            done(act, s_pre, b)
                            if not b.early(RING):
                                act.wait_ge(s_dma[b.slot(RING)], b.uses(RING) * 16)
                            act.activation(
                                spill_out[:, b.slot(RING), :].rearrange("p (g f) -> p g f", f=D),
                                rows[:, b.slot(RING), :, 0:D], ACT.Copy).then_inc(s_packed, 1)
                        pipeline(act, [(0, copy_turned_stage(act, s_turned, s_copied, s_looked)),
                                       (0, penalties)] + ([(2, pack)] if layer == 3 else []))

                    @block.tensor
                    def _(pe):
                        def look(b):
                            done(pe, s_copied, b)
                            free(pe, s_pre, b, 2)
                            if layer == 1:
                                landed(pe, s_dma, b, 16)
                            at = read_base(pe, b) * (D // WINDOW_STEP)
                            for g in range(TILES_PER_BATCH):
                                to = banks[2 + b.slot(2)][:, g * D:(g + 1) * D]
                                last = pe.matmul(to, onehotT[:, b.slot(2), g, :],
                                                 by_chunk[:, bass.ds(at, D)],
                                                 start=True, stop=(layer == 3))
                                if layer == 1:
                                    last = pe.matmul(to, edge_in[0:D_EDGE, b.slot(RING),
                                                                 g * P:(g + 1) * P],
                                                     w1_e[:, :], start=False, stop=True)
                            last.then_inc(s_looked, 1)

                        def turn_masked(b):
                            done(pe, s_masked, b)
                            free(pe, s_max, b, 2)
                            for g in range(TILES_PER_BATCH):
                                last = pe.transpose(banks[4 + b.slot(2)][:, g * P:(g + 1) * P],
                                                    masked[:, b.slot(2), g, :], ident[:, :])
                            last.then_inc(s_mturned, 1)

                        def turn_max(b):
                            done(pe, s_max, b)
                            free(pe, s_rowmax, b, 2)
                            pe.transpose(banks[6 + b.slot(2)][0:1, 0:P],
                                         batch_max[:, b.slot(2):b.slot(2) + 1], ident[:, :])\
                              .then_inc(s_row, 1)
                        pipeline(pe, [(0, turn_stage(pe, s_onehot, s_turned, s_copied)), (1, look),
                                      (2, turn_masked), (3, turn_max)])

                    @block.vector
                    def _(dve):
                        def scores(b):
                            s2, kept = b.slot(2), tiles_of(score, b)
                            looked = banks[2 + s2][:, 0:TILES_PER_BATCH * D].rearrange(
                                "p (g f) -> p g f", f=D)
                            wide = [P, TILES_PER_BATCH, D]
                            done(dve, s_looked, b)
                            landed(dve, s_rows, b, 16 * TILES_PER_BATCH)
                            if layer == 1:
                                dve.tensor_tensor(pre[:, s2, :, :], looked,
                                                  rows[:, b.slot(RING), :, 0:D], ALU.add)\
                                   .then_inc(s_pre, 1)
                                done(dve, s_pre, b)
                                dve.scalar_tensor_tensor(pre[:, s2, :, :], pre[:, s2, :, :], SLOPE,
                                                         pre[:, s2, :, :], ALU.mult, ALU.max)\
                                   .then_inc(s_act, 1)
                                done(dve, s_act, b)
                                dve.tensor_tensor(pre[:, s2, :, :], pre[:, s2, :, :],
                                                  a_w[:, :].unsqueeze(1).to_broadcast(wide),
                                                  ALU.mult).then_inc(s_mul, 1)
                                done(dve, s_mul, b)
                            else:
                                dve.tensor_tensor(pre[:, s2, :, :], looked,
                                                  rows[:, b.slot(RING), :, D:2 * D], ALU.mult)\
                                   .then_inc(s_pre, 1)
                                done(dve, s_pre, b)
                            dve.reduce_sum(small_a[:, s2, :], pre[:, s2, :, :], AX)\
                               .then_inc(s_sum, 1)
                            done(dve, s_sum, b)
                            by, op = (a_b[:, 0:1], ALU.add) if layer == 1 else (ATT_SCALE, ALU.mult)
                            dve.scalar_tensor_tensor(small_b[:, s2, :], small_a[:, s2, :], by,
                                                     tiles_of(in_window, b), op, ALU.mult)\
                               .then_inc(s_valid, 1)
                            done(dve, s_valid, b)
                            dve.tensor_tensor(kept, kept, small_b[:, s2, :], ALU.add)\
                               .then_inc(s_kept, 1)
                            done(dve, s_penalty, b)
                            free(dve, s_mturned, b, 2)
                            full = [P, TILES_PER_BATCH, P]
                            dve.tensor_tensor(masked[:, s2, :, :], penalty[:, s2, :, :],
                                              small_b[:, s2, :].unsqueeze(2).to_broadcast(full),
                                              ALU.add).then_inc(s_masked, 1)

                        def maxima(b):
                            done(dve, s_mturned, b)
                            free(dve, s_row, b, 2)
                            dve.reduce_max(batch_max[:, b.slot(2):b.slot(2) + 1],
                                           banks[4 + b.slot(2)][:, :], AX).then_inc(s_max, 1)

                        def keep_max(b):
                            done(dve, s_row, b)
                            at = accT[0:1, bass.ds(read_base(dve, b), WINDOW)]
                            if not b.early(1):
                                dve.wait_ge(s_rowmax, b.v)
                            dve.tensor_tensor(at, banks[6 + b.slot(2)][0:1, 0:P], at, ALU.max)\
                               .then_inc(s_rowmax, 1)
                        readers = [s_turned, s_penalty]
                        pipeline(dve, [(4, keep_max), (3, maxima),
                                       (0, onehot_stage(dve, s_onehot, readers)), (2, scores)])
            window_loop(name, sweep, True)

        def softmax_sweep(name, n_heads, messages):
            nv = TILES_PER_BATCH * n_heads

            def sweep():
                with Phase(nc, name) as ph:
                    (s_onehot, s_turned, s_copied, s_looked, s_diff, s_clamped, s_exp, s_wa, s_wb,
                     s_sum, s_added) = (ph.sem(n) for n in (
                         "onehot", "turned", "copied", "looked", "diff", "clamped", "exp",
                         "weighted_a", "weighted_b", "summed", "added"))
                    s_msg = [ph.sem(f"msg{n}") for n in range(RING)]
                    block = ph.open()
                    exv = ex[:, :, 0:nv].rearrange("p s (g h) -> p s g h", h=n_heads)
                    weighted = [penalty, masked]
                    sums = [accT, by_chunk]

                    if messages:
                        @block.sync
                        def _(sp):
                            def load(b):
                                free(sp, s_wa, b, RING)
                                free(sp, s_wb, b, RING)
                                sp.dma_start(edge_in[:, b.slot(RING), 0:TILES_PER_BATCH * D],
                                             spill[bass.ds(b.v, 1), :, :].rearrange(
                                                 "o p f -> (o p) f"))\
                                  .then_inc(s_msg[b.slot(RING)], 16)
                            pipeline(sp, [(0, load)])

                    def weigh_stage(eng, which, s_done):
                        def weigh(b):
                            done(eng, s_exp, b)
                            landed(eng, s_msg, b, 16)
                            free(eng, s_sum, b, 2)
                            msg = edge_in[:, b.slot(RING), 0:TILES_PER_BATCH * D].rearrange(
                                "p (g f) -> p g f", f=D)
                            for h in range(2):
                                head = 2 * which + h
                                to = weighted[which][:, b.slot(2), :, h * D:(h + 1) * D]
                                last = eng.tensor_tensor(
                                    to, msg, exv[:, b.slot(RING), :, head:head + 1].to_broadcast(
                                        [P, TILES_PER_BATCH, D]), ALU.mult)
                            last.then_inc(s_done, 1)
                        return weigh

                    if messages:
                        @block.gpsimd
                        def _(pool):
                            pipeline(pool, [(0, weigh_stage(pool, 1, s_wb))])

                    @block.scalar
                    def _(act):
                        def exps(b):
                            done(act, s_clamped, b)
                            free(act, s_sum, b, RING)
                            act.activation(ex[:, b.slot(RING), 0:nv], ex_in[:, b.slot(2), 0:nv],
                                           ACT.Exp).then_inc(s_exp, 1)
                        pipeline(act, [(0, copy_turned_stage(act, s_turned, s_copied, s_looked)),
                                       (1, exps)])

                    @block.tensor
                    def _(pe):
                        def look(b):
                            done(pe, s_copied, b)
                            free(pe, s_diff, b, 2)
                            at = read_base(pe, b)
                            if n_heads * WINDOW_STEP != WINDOW_STEP * N_ACTIVE:
                                at = at // WINDOW_STEP * n_heads
                            else:
                                at = at // (WINDOW_STEP // N_ACTIVE)
                            for g in range(TILES_PER_BATCH):
                                last = pe.matmul(
                                    banks[2 + b.slot(2)][:, g * n_heads:(g + 1) * n_heads],
                                    onehotT[:, b.slot(2), g, :],
                                    small_by_chunk[:, bass.ds(at, n_heads)], start=True, stop=True)
                            last.then_inc(s_looked, 1)

                        def sum_up(b):
                            done(pe, s_exp, b)
                            if messages:
                                done(pe, s_wa, b)
                                done(pe, s_wb, b)
                            free(pe, s_added, b, 1)
                            for which in range(2 if messages else 0):
                                for g in range(TILES_PER_BATCH):
                                    pe.matmul(banks[4 + which][:, 0:P],
                                              weighted[which][:, b.slot(2), g, :],
                                              onehot[:, b.slot(RING), g, :], start=(g == 0),
                                              stop=(g == TILES_PER_BATCH - 1))
                            for g in range(TILES_PER_BATCH):
                                last = pe.matmul(banks[6][0:n_heads, 0:P],
                                                 exv[:, b.slot(RING), g, :],
                                                 onehot[:, b.slot(RING), g, :], start=(g == 0),
                                                 stop=(g == TILES_PER_BATCH - 1))
                            last.then_inc(s_sum, 1)
                        pipeline(pe, [(0, turn_stage(pe, s_onehot, s_turned, s_copied)), (1, look),
                                      (3, sum_up)])

                    @block.vector
                    def _(dve):
                        def diffs(b):
                            s2 = b.slot(2)
                            done(dve, s_looked, b)
                            free(dve, s_exp, b, 2)
                            wide = [P, TILES_PER_BATCH, n_heads]
                            v = ex_in[:, s2, 0:nv]
                            dve.tensor_tensor(
                                v.rearrange("p (g h) -> p g h", h=n_heads),
                                banks[2 + s2][:, 0:nv].rearrange("p (g h) -> p g h", h=n_heads),
                                tiles_of(score, b).unsqueeze(2).to_broadcast(wide), ALU.add)\
                               .then_inc(s_diff, 1)
                            done(dve, s_diff, b)
                            dve.tensor_single_scalar(v, v, 0.0, ALU.min).then_inc(s_clamped, 1)

                        def add(b):
                            done(dve, s_sum, b)
                            at = bass.ds(read_base(dve, b), WINDOW)
                            if not b.early(1):
                                dve.wait_ge(s_added, b.v)
                            for which in range(2 if messages else 0):
                                to = sums[which][:, at]
                                dve.tensor_tensor(to, banks[4 + which][:, 0:P], to, ALU.add)
                            to = featT[0:n_heads, at]
                            dve.tensor_tensor(to, banks[6][0:n_heads, 0:P], to, ALU.add)\
                               .then_inc(s_added, 1)
                        stages = [(4, add), (0, onehot_stage(dve, s_onehot, [s_turned, s_sum])),
                                  (1, diffs)]
                        if messages:
                            stages.append((2, weigh_stage(dve, 0, s_wa)))
                        pipeline(dve, stages)
            window_loop(name, sweep, False)

        layer_norm("norm0", rows_out=True)
        clear("clear0", (accT[:, :], 0.0))
        sum_sweep("sum0", D + D_EDGE, True, False)

        def matmuls0(pe, j, bank, place):
            to = bank[:, place * D:(place + 1) * D]
            at = slice(j * P, (j + 1) * P)
            pe.matmul(to, featT[0:D + 1, at], w0_self[:, :], start=True, stop=False)
            return pe.matmul(to, accT[0:D + D_EDGE, at], w0_agg[:, :], start=False, stop=True)

        def take0(eng, c, n, items, bank):
            to = x[:, items[0]:items[-1] + 1, :]
            return eng.scalar_tensor_tensor(
                to, bank[:, 0:len(items) * D].rearrange("p (j d) -> p j d", d=D), 0.0, to,
                ALU.max, ALU.add)
        take0.both = False
        products("out0", NODE_TILES, BANK // D, matmuls0, take0)

        layer_norm("norm1")

        def matmuls1q(pe, j, bank, place):
            return pe.matmul(bank[:, place * D:(place + 1) * D], featT[0:D + 3, j * P:(j + 1) * P],
                             w1_q[:, :], start=True, stop=True)

        def take1q(eng, c, n, items, bank):
            return copy(eng, edge_in[:, n % RING, 0:len(items) * D], bank[:, 0:len(items) * D])

        def store1q(sp, n, items):
            return sp.dma_start(rows_view(items), edge_in[:, n % RING, 0:len(items) * D].rearrange(
                "p (j d) -> p j d", d=D))
        take1q.both = True
        products("table1q", NODE_TILES, BANK // D, matmuls1q, take1q, store1q)
        table_by_chunk("table1k", w1_k, D)
        clear("clear1", (accT[0:1, :], FAR_BELOW), (score[:, :], 0.0))
        score_sweep("score1", 1)

        def matmuls1m(pe, c, bank, place):
            at = c * WINDOW_STEP
            return pe.matmul(bank[:, place:place + 1], accT[0:1, at:at + P], one[:, :],
                             start=True, stop=True)

        def take1m(eng, c, n, items, bank):
            return eng.tensor_single_scalar(small_by_chunk[:, items[0]:items[-1] + 1],
                                            bank[:, 0:len(items)], -1.0, ALU.mult)
        take1m.both = False
        products("max1", N_CHUNKS, N_CHUNKS, matmuls1m, take1m)

        def matmuls1v(pe, j, bank, place):
            return pe.matmul(bank[:, place * D:(place + 1) * D], featT[0:D + 1, j * P:(j + 1) * P],
                             w1_v[:, :], start=True, stop=True)

        values1 = by_chunk[:, 0:NODE_TILES * D]

        def take1v(eng, c, n, items, bank):
            return copy(eng, values1[:, items[0] * D:(items[-1] + 1) * D], bank[:, 0:len(items) * D])
        take1v.both = True
        products("value1", NODE_TILES, BANK // D, matmuls1v, take1v)
        clear("clear1d", (featT[0:N_ACTIVE, :], 0.0))
        softmax_sweep("soft1", 1, False)

        def matmuls1d(pe, j, bank, place):
            return pe.transpose(bank[:, place:place + 1], featT[0:1, j * P:(j + 1) * P],
                                ident[0:1, 0:1])

        def take1d(eng, c, n, items, bank):
            d = bank[:, 0:NODE_TILES]
            c.do(eng.tensor_single_scalar(node_a[:, :], d, TINY, ALU.max))
            c.do(eng.reciprocal(node_a[:, :], node_a[:, :]))
            c.do(eng.tensor_tensor(node_a[:, :], d, node_a[:, :], ALU.mult))
            v = values1.rearrange("p (j d) -> p j d", d=D)
            c.do(eng.tensor_tensor(v, v, node_a[:, :].unsqueeze(2).to_broadcast([P, NODE_TILES, D]),
                                   ALU.mult))
            return eng.tensor_tensor(x[:, :, :], x[:, :, :], v, ALU.add)
        take1d.both = False
        products("out1", NODE_TILES, NODE_TILES, matmuls1d, take1d)

        layer_norm("norm2", rows_out=True)
        clear("clear2", (accT[:, :], 0.0))
        sum_sweep("sum2", D, False, True)

        def matmuls2(pe, j, bank, place):
            return pe.transpose(bank[:, place * D:(place + 1) * D], accT[0:D, j * P:(j + 1) * P],
                                ident[0:D, 0:D])

        def take2(eng, c, n, items, bank):
            to = x[:, items[0]:items[-1] + 1, :]
            return eng.tensor_tensor(
                to, bank[:, 0:len(items) * D].rearrange("p (j d) -> p j d", d=D), to, ALU.add)
        take2.both = False
        products("out2", NODE_TILES, BANK // D, matmuls2, take2)

        layer_norm("norm3")
        with Phase(nc, "weights3") as ph:
            s_chain, s_rel, s_pe, s_t, s_key, s_copied, s_zero, s_bias = (
                ph.sem(n) for n in ("chain", "rel", "pe", "turned", "key", "copied", "zero",
                                    "bias"))
            block = ph.open()

            @block.sync
            def _(sp):
                sp.wait_ge(s_zero, 1)
                sp.dma_start(w3_table[D + 1:D + 2, :, D:2 * D],
                             a["w3_bk"].rearrange("i (r o) -> i r o", o=D)).then_inc(s_bias, 16)
                sp.wait_ge(s_bias, 16)

            @block.vector
            def _(dve):
                c = Chain(dve, s_chain)
                dve.memset(w3_table[D:D + 2, :, :], 0.0).then_inc(s_zero, 1)
                c.do(dve.reduce_sum(rel_mean[:, :], w3_rel[:, :, :], AX))
                dve.tensor_single_scalar(rel_mean[:, :], rel_mean[:, :], 1.0 / D, ALU.mult)\
                   .then_inc(s_rel, 1)
                dve.tensor_copy(w3_table[0:D, :, 0:D], w3_rel[:, :, :]).then_inc(s_copied, 1)
                for r in range(N_REL):
                    dve.tensor_copy(w3_table[0:D, r, D:2 * D], w3_k[:, 0, :]).then_inc(s_copied, 1)
                dve.wait_ge(s_pe, 1)
                dve.wait_ge(s_zero, 1)
                dve.tensor_copy(w3_table[D:D + 1, :, D:2 * D],
                                banks[0][0:1, :].rearrange("p (r o) -> p r o", o=D))\
                   .then_inc(s_copied, 1)
                dve.wait_ge(s_pe, 2)
                dve.tensor_copy(rulesT[:, :], banks[1][0:D, 0:N_ACTIVE]).then_inc(s_t, 1)
                dve.wait_ge(s_pe, 3)
                dve.tensor_copy(rule_keyT[:, :], banks[2][0:D, 0:N_ACTIVE]).then_inc(s_key, 1)
                dve.wait_ge(s_pe, 4)
                dve.tensor_copy(w3_rule[:, :], banks[3][0:D + 1, 0:N_ACTIVE]).then_inc(s_copied, 1)
                dve.wait_ge(s_copied, 3 + N_REL)

            @block.tensor
            def _(pe):
                pe.wait_ge(s_rel, 1)
                for r in range(N_REL):
                    last = pe.matmul(banks[0][0:1, r * D:(r + 1) * D], rel_mean[:, r:r + 1],
                                     w3_k[:, 1, :], start=True, stop=True)
                last.then_inc(s_pe, 1)
                pe.transpose(banks[1][0:D, 0:N_ACTIVE], rules[:, :],
                             ident[0:N_ACTIVE, 0:N_ACTIVE]).then_inc(s_pe, 1)
                pe.wait_ge(s_t, 1)
                pe.matmul(banks[2][0:D, 0:N_ACTIVE], w3_k[:, 2, :], rulesT[:, :], start=True,
                          stop=True).then_inc(s_pe, 1)
                pe.wait_ge(s_key, 1)
                pe.matmul(banks[3][0:D + 1, 0:N_ACTIVE], w3_qT[:, :], rule_keyT[:, :], start=True,
                          stop=True).then_inc(s_pe, 1)

        half_cols = N_REL * 2 * D // 2
        table_cols = w3_table[:, :, :].rearrange("i r o -> i (r o)")
        rel_rows_v = rel_rows.rearrange("(j p r) o -> j p (r o)", p=P, r=N_REL)

        def matmuls3t(pe, item, bank, place):
            j, half = divmod(item, 2)
            return pe.matmul(bank[:, :], featT[0:D + 2, j * P:(j + 1) * P],
                             table_cols[:, half * half_cols:(half + 1) * half_cols],
                             start=True, stop=True)

        def take3t(eng, c, n, items, bank):
            return copy(eng, edge_in[:, n % RING, :], bank[:, :])

        def store3t(sp, n, items):
            j, half = divmod(items[0], 2)
            return sp.dma_start(rel_rows_v[j, :, half * half_cols:(half + 1) * half_cols],
                                edge_in[:, n % RING, :])
        take3t.both = True
        products("table3", 2 * NODE_TILES, 1, matmuls3t, take3t, store3t)
        table_by_chunk("table3q", w3_q, D + 1)
        clear("clear3", (accT[0:1, :], FAR_BELOW), (score[:, :], 0.0))
        score_sweep("score3", 3)

        def matmuls3m(pe, c, bank, place):
            at = c * WINDOW_STEP
            w = N_ACTIVE + 1
            pe.matmul(bank[:, place * w:place * w + N_ACTIVE], featT[0:D + 1, at:at + P],
                      w3_rule[:, :], start=True, stop=True)
            return pe.matmul(bank[:, place * w + N_ACTIVE:(place + 1) * w], accT[0:1, at:at + P],
                             one[:, :], start=True, stop=True)

        def take3m(eng, c, n, items, bank):
            k = len(items)
            v = bank[:, 0:k * (N_ACTIVE + 1)].rearrange("p (c r) -> p c r", r=N_ACTIVE + 1)
            rule_score = pre[:, 0, :, :].rearrange("p g f -> p (g f)")[:, 0:k * N_ACTIVE]\
                .rearrange("p (c r) -> p c r", r=N_ACTIVE)
            base_max = node_b[:, 0:k]
            to = small_by_chunk[:, items[0] * N_ACTIVE:(items[-1] + 1) * N_ACTIVE].rearrange(
                "p (c r) -> p c r", r=N_ACTIVE)
            c.do(eng.tensor_single_scalar(rule_score, v[:, :, 0:N_ACTIVE], ATT_SCALE, ALU.mult))
            c.do(eng.tensor_copy(base_max, v[:, :, N_ACTIVE]))
            c.do(eng.tensor_tensor(to, rule_score,
                                   base_max.unsqueeze(2).to_broadcast([P, k, N_ACTIVE]), ALU.add))
            return eng.tensor_tensor(to, rule_score, to, ALU.subtract)
        take3m.both = False
        products("max3", N_CHUNKS, 50, matmuls3m, take3m)
        clear("clear3d", (featT[0:N_ACTIVE, :], 0.0), (accT[:, :], 0.0),
              (by_chunk[:, 0:N_PAD], 0.0))
        softmax_sweep("soft3", N_ACTIVE, True)

        def matmuls3d(pe, j, bank, place):
            return pe.transpose(bank[:, place * N_ACTIVE:(place + 1) * N_ACTIVE],
                                featT[0:N_ACTIVE, j * P:(j + 1) * P], ident[0:N_ACTIVE, 0:N_ACTIVE])

        denom = small_by_chunk[:, 0:NODE_TILES * N_ACTIVE]

        def take3d(eng, c, n, items, bank):
            c.do(eng.tensor_single_scalar(denom, bank[:, 0:NODE_TILES * N_ACTIVE], TINY, ALU.max))
            c.do(eng.reciprocal(denom, denom))
            return eng.tensor_single_scalar(denom, denom, 1.0 / N_ACTIVE, ALU.mult)
        take3d.both = False
        products("denom3", NODE_TILES, NODE_TILES, matmuls3d, take3d)

        def matmuls3o(pe, j, bank, place):
            pe.transpose(bank[:, 0:P], accT[:, j * P:(j + 1) * P], ident[:, :])
            return pe.transpose(bank[:, P:2 * P], by_chunk[:, j * P:(j + 1) * P], ident[:, :])

        message3 = featT[:, 0:NODE_TILES * D].rearrange("p (j d) -> p j d", d=D)

        def take3o(eng, c, n, items, bank):
            j = items[0]
            tmp = rows[:, n % RING, :, 0:D]
            c.do(eng.tensor_tensor(
                tmp, bank[:, 0:2 * P].rearrange("p (h d) -> p h d", d=D),
                denom[:, j * N_ACTIVE:(j + 1) * N_ACTIVE].unsqueeze(2).to_broadcast(
                    [P, N_ACTIVE, D]), ALU.mult))
            return eng.reduce_sum(message3[:, j, :], tmp.rearrange("p h d -> p d h"), AX)
        take3o.both = False
        products("mean3", NODE_TILES, 1, matmuls3o, take3o)

        with Phase(nc, "out3") as ph:
            s_chain, s_var, s_std, s_out, s_x = (
                ph.sem(n) for n in ("chain", "var", "std", "out", "x"))
            block = ph.open()

            @block.vector
            def _(dve):
                c = Chain(dve, s_chain)
                wide = [P, NODE_TILES, D]

                def vec(n):
                    return bias3[:, n:n + 1, :].to_broadcast(wide)
                c.do(dve.tensor_tensor(message3, message3, vec(0), ALU.add))
                c.do(dve.reduce_sum(node_a[:, :], message3, AX))
                c.do(dve.tensor_single_scalar(node_a[:, :], node_a[:, :], 1.0 / D, ALU.mult))
                c.do(dve.tensor_tensor(message3, message3,
                                       node_a[:, :].unsqueeze(2).to_broadcast(wide), ALU.subtract))
                c.do(dve.tensor_tensor(centred, message3, message3, ALU.mult))
                c.do(dve.reduce_sum(node_a[:, :], centred, AX))
                dve.tensor_scalar(node_a[:, :], node_a[:, :], 1.0 / D, LN_EPS, ALU.mult, ALU.add)\
                   .then_inc(s_var, 1)
                dve.wait_ge(s_std, 1)
                c.do(dve.reciprocal(node_b[:, :], node_b[:, :]))
                c.do(dve.tensor_tensor(message3, message3,
                                       node_b[:, :].unsqueeze(2).to_broadcast(wide), ALU.mult))
                c.do(dve.tensor_tensor(message3, message3, vec(1), ALU.mult))
                c.do(dve.tensor_tensor(message3, message3, vec(2), ALU.add))
                dve.scalar_tensor_tensor(x[:, :, :], message3, 0.0, x[:, :, :], ALU.max, ALU.add)\
                   .then_inc(s_x, 1)

            @block.scalar
            def _(act):
                act.wait_ge(s_var, 1)
                act.activation(node_b[:, :], node_a[:, :], ACT.Sqrt).then_inc(s_std, 1)

            @block.sync
            def _(sp):
                sp.wait_ge(s_x, 1)
                sp.dma_start(out, x[:, :, :].rearrange("p j d -> p (j d)")).then_inc(s_out, 16)
                sp.wait_ge(s_out, 16)


def kernel(**inputs):
    import concourse.bacc as bacc
    from concourse.bass_utils import run_bass_kernel_spmd

    def arr(name):
        return np.asarray(inputs[name])

    def edge_major(v, fill):
        return np.pad(v, (0, E_PAD - N_EDGES), constant_values=fill).reshape(N_TILES, P).T

    def row(v):
        return v.reshape(1, -1)

    dst = np.pad(arr("dst"), (0, E_PAD - N_EDGES), constant_values=N_NODES)
    ea = np.pad(arr("edge_attr_32"), ((0, E_PAD - N_EDGES), (0, 0)))
    w0 = arr("L0_gnn_W").T
    wq3, bq3 = arr("L3_gnn_Wq_w"), row(arr("L3_gnn_Wq_bias"))
    arrays = {
        "x_l": np.pad(arr("x"), ((0, N_PAD - N_NODES), (0, 0))).reshape(NODE_TILES, P, D)
        .transpose(1, 0, 2).reshape(P, NODE_TILES * D),
        "src_l": edge_major(arr("src"), 0),
        "dst_l": dst.reshape(N_TILES, P).T,
        "dst_b": dst.reshape(BATCH_ROWS, 4 * BATCH),
        "type_l": edge_major(arr("edge_type_8"), 0),
        "w_l": edge_major(arr("edge_weight"), 0),
        "w2_l": edge_major(arr("edge_weight_n2"), 0),
        "ea_l": ea.reshape(N_TILES, P, D_EDGE).transpose(1, 0, 2).reshape(P, N_TILES * D_EDGE),
        "eaT_l": ea.T,
        "w0_self": np.concatenate([w0[0:D], row(arr("L0_gnn_b"))]),
        "w0_agg": w0[D:],
        "w1_q": np.concatenate([arr("L1_gnn_W_q"), row(arr("L1_gnn_b_q")), row(arr("L1_gnn_b_k")),
                                row(arr("L1_gnn_b_e"))]),
        "w1_k": arr("L1_gnn_W_k"),
        "w1_v": np.concatenate([arr("L1_gnn_W_v"), row(arr("L1_gnn_b_v"))]),
        "w1_e": arr("L1_gnn_W_e"),
        "a_w": row(arr("L1_gnn_a_w")),
        "a_b": row(arr("L1_gnn_a_b")),
        "w3_rel": arr("L3_gnn_W_r").transpose(1, 0, 2).reshape(D, N_REL * D),
        "w3_q": np.concatenate([wq3, bq3]),
        "w3_qT": np.concatenate([wq3, bq3]).T,
        "w3_k": arr("L3_gnn_Wk_w").reshape(3, D, D).transpose(1, 0, 2).reshape(D, 3 * D),
        "w3_bk": np.tile(row(arr("L3_gnn_Wk_bias")), (1, N_REL)),
        "rule_ids": arr("L3_gnn_rule_ids").reshape(N_ACTIVE, 1),
        "rule_emb": arr("L3_gnn_rule_emb"),
        "bias3": np.concatenate([row(arr("L3_gnn_bias")), row(arr("L3_gnn_ln_g")),
                                 row(arr("L3_gnn_ln_b"))], axis=1),
    }
    arrays = {k: np.ascontiguousarray(v) for k, v in arrays.items()}
    nc = bacc.Bacc("TRN2", target_bir_lowering=False, num_devices=1)
    aps = {k: nc.dram_tensor("in_" + k, v.shape, mybir.dt.from_np(v.dtype), kind="ExternalInput").ap()
           for k, v in arrays.items()}
    out = nc.dram_tensor("out", (P, NODE_TILES * D), F32, kind="ExternalOutput").ap()
    graph_layers(nc, aps, out)
    r = run_bass_kernel_spmd(nc, [{"in_" + k: v for k, v in arrays.items()}], core_ids=[0])
    got = np.asarray(r.results[0]["out"])
    return got.reshape(P, NODE_TILES, D).transpose(1, 0, 2).reshape(N_PAD, D)[:N_NODES]
```

```python
import contextlib

import numpy as np

import concourse.bass as bass
from concourse import mybir

F32 = mybir.dt.float32
BF16 = mybir.dt.bfloat16
I32 = mybir.dt.int32
ALU = mybir.AluOpType
ACT = mybir.ActivationFunctionType
AX = mybir.AxisListType.X

P = 128
N_NODES, N_EDGES, D, D_EDGE = 6250, 200000, 64, 32
N_REL, N_ACTIVE = 8, 4
LN_EPS = 1e-5
SLOPE = 0.2
ATT_SCALE = 1.0 / D ** 0.5
FAR_BELOW = -1.0e30
TINY = 1.0e-30

TILES_PER_BATCH = 4
BATCH = TILES_PER_BATCH * P
UNROLL = 8
N_BATCHES = -(-N_EDGES // (BATCH * UNROLL)) * UNROLL
N_TILES = N_BATCHES * TILES_PER_BATCH
E_PAD = N_BATCHES * BATCH
BATCH_ROWS = N_BATCHES // 4

NODE_TILES = -(-(N_NODES + 1) // P) + 1
N_PAD = NODE_TILES * P
WINDOW, WINDOW_STEP = 128, 32
LAST_BASE = N_PAD - WINDOW
N_CHUNKS = LAST_BASE // WINDOW_STEP + 1
RING = 4
ONEHOT_RING = 8
BANK = 512
PARTS = 3


class Batch:

    def __init__(self, i, off):
        self.i, self.off = i, off
        self.v = off if i is None else i * UNROLL + off

    def slot(self, ring):
        return self.off % ring

    def uses(self, ring):
        return self.off // ring if self.i is None else self.i * (UNROLL // ring) + self.off // ring

    def early(self, ring):
        return self.i is None and self.off < ring

    def of_next_group(self):
        b = Batch(self.i, self.off - self.off % RING + RING)
        return b if self.i is not None or b.off < N_BATCHES else None


def done(eng, sem, b):
    eng.wait_ge(sem, b.v + 1)


def free(eng, sem, b, ring):
    if not b.early(ring):
        eng.wait_ge(sem, b.v + (1 - ring))


def landed(eng, sems, b, per_use):
    eng.wait_ge(sems[b.slot(RING)], (b.uses(RING) + 1) * per_use)


def pipeline(eng, stages):
    def step(i, t):
        for lag, stage in stages:
            b = t - lag
            if i is not None or 0 <= b < N_BATCHES:
                stage(Batch(i, b))
    last = N_BATCHES // UNROLL - 1
    for t in range(2 * UNROLL):
        step(None, t)
    with eng.Fori(2, last) as i:
        for u in range(UNROLL):
            step(i, u)
    for t in range(last * UNROLL, N_BATCHES + max(lag for lag, _ in stages)):
        step(None, t)


class Phase:

    def __init__(self, nc, name):
        self.nc, self.name, self.sems, self.shared = nc, name, [], []
        self.stack = contextlib.ExitStack()

    def sem(self, what):
        s = self.stack.enter_context(self.nc.semaphore(f"{self.name}_{what}"))
        self.sems.append(s)
        return s

    def use(self, sems):
        self.shared = sems
        return sems

    def __enter__(self):
        self.block_stack = contextlib.ExitStack()
        return self

    def open(self):
        return self.block_stack.enter_context(self.nc.Block())

    def __exit__(self, *error):
        self.block_stack.__exit__(*error)
        if error[0] is None:
            nums = [s.num for s in self.sems]
            self.nc.all_engine_barrier(sems_to_clear=range(min(nums), max(nums) + 1))
            if self.shared:
                nums = [s.num for s in self.shared]
                self.nc.all_engine_barrier(sems_to_clear=range(min(nums), max(nums) + 1))
        self.stack.__exit__(*error)
        return False


class Chain:

    def __init__(self, eng, sem):
        self.eng, self.sem, self.n = eng, sem, 0

    def do(self, ins):
        self.n += 1
        ins.then_inc(self.sem, 1)
        self.eng.wait_ge(self.sem, self.n)


def graph_layers(nc, a, out):
    ctx = contextlib.ExitStack()
    with ctx:
        def sb(name, shape, dt=F32):
            return ctx.enter_context(nc.sbuf_tensor(name, shape, dt))

        node_rows = nc.dram_tensor("node_rows", (N_PAD, D), F32).ap()
        rel_rows = nc.dram_tensor("rel_rows", (N_PAD * N_REL, 2 * D), F32).ap()
        spill = nc.dram_tensor("spill", (N_BATCHES, P, TILES_PER_BATCH * D), F32).ap()
        batch_facts = nc.dram_tensor("batch_facts", (2, N_BATCHES), I32).ap()

        ident = sb("ident", [P, P])
        iota = sb("iota", [P, P])
        one = sb("one", [P, 1])
        ident_b = sb("ident_b", [P, P], BF16)

        src_idx = sb("src_idx", [P, N_TILES], I32)
        rel_idx = sb("rel_idx", [P, N_TILES], I32)
        dst_rel0 = sb("dst_rel0", [P, N_TILES])
        dst_rel = sb("dst_rel", [P, N_TILES])
        weight = sb("weight", [P, N_TILES])
        score = sb("score", [P, N_TILES])
        fresh = sb("fresh", [P, N_TILES])
        fresh_slots = sb("fresh_slots", [P, 2 * RING, TILES_PER_BATCH])

        bases = sb("bases", [33, N_BATCHES], I32)
        base0 = bases[32:33, :]
        base = bases[0:1, :]
        n_windows = sb("n_windows", [1, 1], I32)

        x = sb("x", [P, NODE_TILES, D])
        featT = sb("featT", [P, N_PAD])
        accT = sb("accT", [P, N_PAD])
        by_chunk = sb("by_chunk", [P, N_CHUNKS * D])
        small_by_chunk = sb("small_by_chunk", [P, N_CHUNKS * PARTS * N_ACTIVE], BF16)
        max_row = featT[96:97, :]
        table_01 = by_chunk[:, :].bitcast(BF16).rearrange("p (c s d) -> p c s d", s=2, d=D)
        table_2 = accT[:, 0:N_CHUNKS * D // 2].bitcast(BF16)
        node_a = sb("node_a", [P, NODE_TILES])
        node_b = sb("node_b", [P, NODE_TILES])
        centred = by_chunk[:, 0:NODE_TILES * D].rearrange("p (j d) -> p j d", d=D)
        normed = by_chunk[:, NODE_TILES * D:2 * NODE_TILES * D].rearrange("p (j d) -> p j d", d=D)

        idx_slots = sb("idx_slots", [P, 2, RING * TILES_PER_BATCH], I32)
        rows = sb("rows", [P, RING, TILES_PER_BATCH, 2 * D])
        onehot_b = sb("onehot_b", [P, ONEHOT_RING, TILES_PER_BATCH, P], BF16)
        onehotT = sb("onehotT", [P, 2, TILES_PER_BATCH, P], BF16)
        onehot = sb("onehot", [P, RING, TILES_PER_BATCH, P])
        penalty, masked = onehot[:, 0:2, :, :], onehot[:, 2:4, :, :]
        edge_in = sb("edge_in", [P, RING, BANK])
        spill_out = edge_in[:, :, 0:TILES_PER_BATCH * D]
        pre = sb("pre", [P, 2, TILES_PER_BATCH, D])
        products_out = sb("products_out", [P, TILES_PER_BATCH, D])
        batch_max = sb("batch_max", [P, 2])
        ex_in = sb("ex_in", [P, 2, TILES_PER_BATCH * N_ACTIVE])
        ex = sb("ex", [P, RING, TILES_PER_BATCH * N_ACTIVE])
        ex_left = sb("ex_left", [P, 2, TILES_PER_BATCH])
        ex_parts = sb("ex_parts", [P, RING, TILES_PER_BATCH, PARTS], BF16)

        w0_self = sb("w0_self", [D + 1, D])
        w0_agg = sb("w0_agg", [D + D_EDGE, D])
        w1_q = sb("w1_q", [D + 3, D])
        w1_k = sb("w1_k", [D, D])
        w1_v = sb("w1_v", [D + 1, D])
        w1_e = sb("w1_e", [D_EDGE, D])
        a_w = sb("a_w", [P, D])
        a_b = sb("a_b", [P, 1])
        w3_rel = sb("w3_rel", [D, N_REL, D])
        w3_q = sb("w3_q", [D + 1, D])
        w3_qT = sb("w3_qT", [D, D + 1])
        w3_k = sb("w3_k", [D, 3, D])
        w3_table = penalty[0:D + 2, :, :, :].rearrange("p s g n -> p (s g) n")
        rel_mean = sb("rel_mean", [D, N_REL])
        rule_ids = sb("rule_ids", [N_ACTIVE, 1], I32)
        rules = sb("rules", [N_ACTIVE, D])
        rulesT = sb("rulesT", [D, N_ACTIVE])
        rule_keyT = sb("rule_keyT", [D, N_ACTIVE])
        w3_rule = sb("w3_rule", [D + 1, N_ACTIVE])
        bias3 = sb("bias3", [P, 3, D])

        gather_sems = [ctx.enter_context(nc.semaphore(f"gathered{n}")) for n in range(RING)]
        s_rules = ctx.enter_context(nc.semaphore("gathered_rules"))

        banks = [ctx.enter_context(nc.psum_tensor(f"bank{n}", [P, BANK], F32)) for n in range(8)]

        dst_rows = accT[0:BATCH_ROWS, 0:4 * BATCH].bitcast(I32)
        dst_rows_f = featT[0:BATCH_ROWS, 0:4 * BATCH]
        dst_raw = rel_idx
        fact_i = idx_slots[0:BATCH_ROWS, 0, :]
        base_wide = penalty[:, 0, :, :].rearrange("p g n -> p (g n)")[:, 0:N_BATCHES].bitcast(I32)
        base_wide_f = masked[:, 0, :, :].rearrange("p g n -> p (g n)")[:, 0:N_BATCHES]
        with Phase(nc, "load") as ph:
            s_dst, s_in, s_w, s_const = (ph.sem(n) for n in ("dst", "edges", "weights", "consts"))
            s_chain, s_fact, s_back, s_rule = (
                ph.sem(n) for n in ("chain", "fact", "back", "rule"))
            block = ph.open()
            edge_loads = [(dst_raw[:, :], a["dst_l"]), (src_idx[:, :], a["src_l"]),
                          (score[:, :], a["w2_l"]), (weight[:, :], a["w_l"]),
                          (fresh[:, :].bitcast(I32), a["type_l"]),
                          (x[:, :, :].rearrange("p j d -> p (j d)"), a["x_l"])]
            weight_loads = [(w0_self, a["w0_self"]), (w0_agg, a["w0_agg"]), (w1_q, a["w1_q"]),
                            (w1_k, a["w1_k"]), (w1_v, a["w1_v"]), (w1_e, a["w1_e"]),
                            (w3_q, a["w3_q"]), (w3_qT, a["w3_qT"]),
                            (w3_rel, a["w3_rel"].rearrange("i (r o) -> i r o", o=D)),
                            (w3_k, a["w3_k"].rearrange("i (r o) -> i r o", o=D))]

            @block.sync
            def _(sp):
                sp.dma_start(dst_rows, a["dst_b"]).then_inc(s_dst, 16)
                for to, of in edge_loads:
                    sp.dma_start(to, of).then_inc(s_in, 16)
                sp.wait_ge(s_fact, 1)
                sp.dma_start(batch_facts.rearrange("f (p q) -> p f q", q=4),
                             fact_i[:, 0:8].rearrange("p (f q) -> p f q", q=4)).then_inc(s_back, 16)
                sp.wait_ge(s_back, 16)
                sp.dma_start(base0[:, :], batch_facts[0:1, :]).then_inc(s_back, 16)
                sp.dma_start(base[:, :], batch_facts[1:2, :]).then_inc(s_back, 16)
                sp.dma_start(base_wide, batch_facts[0:1, :].to_broadcast([P, N_BATCHES]))\
                  .then_inc(s_back, 16)

            @block.scalar
            def _(act):
                for to, of in weight_loads:
                    act.dma_start(to[:], of).then_inc(s_w, 16)
                act.dma_start(a_w[:, :], a["a_w"].to_broadcast([P, D])).then_inc(s_w, 16)
                act.dma_start(a_b[:, :], a["a_b"].to_broadcast([P, 1])).then_inc(s_w, 16)
                act.dma_start(bias3[:, :, :].rearrange("p r o -> p (r o)"),
                              a["bias3"].to_broadcast([P, 3 * D])).then_inc(s_w, 16)
                act.dma_start(rule_ids[:, :], a["rule_ids"]).then_inc(s_rule, 16)
                act.wait_ge(s_w, 16 * (len(weight_loads) + 3))

            @block.gpsimd
            def _(pool):
                pool.memset(ident[:, :], 0.0).then_inc(s_const, 1)
                pool.iota(iota[:, :], [[1, P]], base=0, channel_multiplier=0,
                          allow_small_or_imprecise_dtypes=True).then_inc(s_const, 1)
                pool.memset(one[:, :], 1.0).then_inc(s_const, 1)
                pool.memset(ident_b[:, :], 0.0).then_inc(s_const, 1)
                pool.wait_ge(s_const, 4)
                for m in (ident, ident_b):
                    pool.affine_select(out=m[:, :], in_=m[:, :], compare_op=ALU.not_equal,
                                       fill=1.0, base=0, pattern=[[-1, P]], channel_multiplier=1)\
                        .then_inc(s_const, 1)
                pool.wait_ge(s_rule, 16)
                pool.indirect_dma_start(
                    out=rules[:, :], out_offset=None, in_=a["rule_emb"],
                    in_offset=bass.IndirectOffsetOnAxis(ap=rule_ids[:, 0:1], axis=0))\
                    .then_inc(s_rules, 16)
                pool.wait_ge(s_rules, 16)

            @block.vector
            def _(dve):
                c = Chain(dve, s_chain)
                least, most = node_a[0:BATCH_ROWS, 0:4], node_a[0:BATCH_ROWS, 4:8]
                dve.wait_ge(s_dst, 16)
                rows4 = dst_rows_f.rearrange("p (q e) -> p q e", q=4)
                c.do(dve.tensor_copy(dst_rows_f, dst_rows))
                c.do(dve.tensor_reduce(least, rows4, AX, ALU.min))
                c.do(dve.tensor_reduce(most, rows4, AX, ALU.max))
                c.do(dve.tensor_copy(fact_i[:, 0:4], least))
                c.do(dve.tensor_copy(fact_i[:, 4:8], most))
                c.do(dve.tensor_single_scalar(fact_i[:, 0:4], fact_i[:, 0:4],
                                              WINDOW_STEP.bit_length() - 1,
                                              ALU.arith_shift_right))
                c.do(dve.tensor_single_scalar(fact_i[:, 0:4], fact_i[:, 0:4], WINDOW_STEP, ALU.mult))
                c.do(dve.tensor_tensor(fact_i[:, 4:8], fact_i[:, 4:8], fact_i[:, 0:4], ALU.subtract))
                dve.tensor_single_scalar(fact_i[:, 4:8], fact_i[:, 4:8], WINDOW.bit_length() - 1,
                                         ALU.arith_shift_right).then_inc(s_fact, 1)
                dve.memset(featT[64:96, :], 1.0).then_inc(s_fact, 1)
                dve.wait_ge(s_back, 64)
                c.do(dve.tensor_reduce(n_windows[:, :], base[:, :], AX, ALU.max))
                c.do(dve.tensor_single_scalar(n_windows[:, :], n_windows[:, :], 1, ALU.add))
                c.do(dve.tensor_copy(base_wide_f, base_wide))
                dve.wait_ge(s_in, 16 * len(edge_loads))
                c.do(dve.tensor_copy(dst_rel0[:, :], dst_raw[:, :]))
                by_batch = dst_rel0[:, :].rearrange("p (b g) -> p b g", g=TILES_PER_BATCH)
                c.do(dve.tensor_tensor(by_batch, by_batch, base_wide_f.unsqueeze(2).to_broadcast(
                    [P, N_BATCHES, TILES_PER_BATCH]), ALU.subtract))
                c.do(dve.tensor_single_scalar(rel_idx[:, :], src_idx[:, :], N_REL, ALU.mult))
                c.do(dve.tensor_tensor(rel_idx[:, :], rel_idx[:, :],
                                       fresh[:, :].bitcast(I32), ALU.add))
                c.do(dve.tensor_tensor(weight[:, :], score[:, :], weight[:, :], ALU.mult))

        def layer_norm(name, rows_out=False):
            with Phase(nc, name) as ph:
                s_chain, s_var, s_std, s_h, s_t, s_ev, s_out = (
                    ph.sem(n) for n in ("chain", "var", "std", "normed", "turned", "copied", "out"))
                block = ph.open()
                groups = [(g, min(4, NODE_TILES - g)) for g in range(0, NODE_TILES, 4)]

                @block.vector
                def _(dve):
                    c = Chain(dve, s_chain)
                    wide = [P, NODE_TILES, D]
                    c.do(dve.reduce_sum(node_a[:, :], x[:, :, :], AX))
                    c.do(dve.tensor_single_scalar(node_a[:, :], node_a[:, :], 1.0 / D, ALU.mult))
                    c.do(dve.tensor_tensor(centred, x[:, :, :],
                                           node_a[:, :].unsqueeze(2).to_broadcast(wide), ALU.subtract))
                    c.do(dve.tensor_tensor(normed, centred, centred, ALU.mult))
                    c.do(dve.reduce_sum(node_a[:, :], normed, AX))
                    dve.tensor_scalar(node_a[:, :], node_a[:, :], 1.0 / D, LN_EPS, ALU.mult, ALU.add)\
                       .then_inc(s_var, 1)
                    dve.wait_ge(s_std, 1)
                    c.do(dve.reciprocal(node_b[:, :], node_b[:, :]))
                    dve.scalar_tensor_tensor(normed, centred, 0.0,
                                             node_b[:, :].unsqueeze(2).to_broadcast(wide),
                                             ALU.max, ALU.mult).then_inc(s_h, 1)

                @block.scalar
                def _(act):
                    act.wait_ge(s_var, 1)
                    act.activation(node_b[:, :], node_a[:, :], ACT.Sqrt).then_inc(s_std, 1)
                    for n, (g, k) in enumerate(groups):
                        act.wait_ge(s_t, n + 1)
                        act.activation(featT[0:D, g * P:(g + k) * P], banks[n % 4][0:D, 0:k * P],
                                       ACT.Copy).then_inc(s_ev, 1)

                @block.tensor
                def _(pe):
                    pe.wait_ge(s_h, 1)
                    for n, (g, k) in enumerate(groups):
                        if n >= 4:
                            pe.wait_ge(s_ev, n - 3)
                        for j in range(k):
                            last = pe.transpose(banks[n % 4][0:D, j * P:(j + 1) * P],
                                                normed[:, g + j, :], ident[:, :])
                        last.then_inc(s_t, 1)

                @block.sync
                def _(sp):
                    if rows_out:
                        sp.wait_ge(s_h, 1)
                        sp.dma_start(node_rows.rearrange("(j p) d -> p j d", p=P), normed)\
                          .then_inc(s_out, 16)
                        sp.wait_ge(s_out, 16)

        def products(name, n_items, per_bank, matmuls, take, stores=None):
            both = take.both
            with Phase(nc, name) as ph:
                s_pe, s_chain = ph.sem("filled"), ph.sem("chain")
                s_took = [ph.sem("took_dve"), ph.sem("took_act")]
                s_store = [ph.sem(f"store{n}") for n in range(RING)]
                block = ph.open()
                groups = [range(g, min(g + per_bank, n_items)) for g in range(0, n_items, per_bank)]
                who = [n % 2 if both else 0 for n in range(len(groups))]

                def taken(eng, n):
                    eng.wait_ge(s_took[who[n]], sum(w == who[n] for w in who[:n + 1]))

                @block.tensor
                def _(pe):
                    for n, items in enumerate(groups):
                        if n >= RING:
                            taken(pe, n - RING)
                        for place, item in enumerate(items):
                            last = matmuls(pe, item, banks[n % RING], place)
                        last.then_inc(s_pe, 1)

                def emptier(me):
                    def run(eng):
                        c = Chain(eng, s_chain) if me == 0 else None
                        for n, items in enumerate(groups):
                            if who[n] != me:
                                continue
                            eng.wait_ge(s_pe, n + 1)
                            if stores and n >= RING:
                                eng.wait_ge(s_store[n % RING], 16 * (n // RING))
                            if not both and n:
                                taken(eng, n - 1)
                            take(eng, c, n, items, banks[n % RING]).then_inc(s_took[me], 1)
                    return run
                block.vector(emptier(0))
                if both:
                    block.scalar(emptier(1))
                if stores:
                    @block.sync
                    def _(sp):
                        for n, items in enumerate(groups):
                            taken(sp, n)
                            stores(sp, n, items).then_inc(s_store[n % RING], 16)
                        for k in range(min(RING, len(groups))):
                            sp.wait_ge(s_store[k], 16 * len(range(k, len(groups), RING)))

        def copy(eng, to, of):
            if eng is nc.scalar:
                return eng.activation(to, of, ACT.Copy)
            return eng.tensor_copy(to, of)

        def split(eng, c, value, left, parts):
            c.do(eng.tensor_copy(parts[0], value))
            c.do(eng.tensor_tensor(left, value, parts[0], ALU.subtract))
            c.do(eng.tensor_copy(parts[1], left))
            return eng.tensor_tensor(parts[2], left, parts[1], ALU.subtract)

        def table_by_chunk(name, w, k_rows):
            def matmuls(pe, c, bank, place):
                at = c * WINDOW_STEP
                return pe.matmul(bank[:, place * D:(place + 1) * D], featT[0:k_rows, at:at + P],
                                 w[:, :], start=True, stop=True)

            def take(eng, c, n, items, bank):
                k = len(items)
                chunks = slice(items[0], items[-1] + 1)
                left = rows[:, n % RING, :, :].rearrange("p g f -> p (g f)")[:, 0:k * D]\
                    .rearrange("p (c d) -> p c d", d=D)
                parts = [table_01[:, chunks, 0, :], table_01[:, chunks, 1, :],
                         table_2[:, items[0] * D:(items[-1] + 1) * D].rearrange(
                             "p (c d) -> p c d", d=D)]
                return split(eng, c, bank[:, 0:k * D].rearrange("p (c d) -> p c d", d=D), left,
                             parts)
            take.both = False
            products(name, N_CHUNKS, BANK // D, matmuls, take)

        def rows_view(items):
            return node_rows[items[0] * P:(items[-1] + 1) * P, :].rearrange("(j p) d -> p j d", p=P)

        def gather_stage(pool, indices, table, width, s_rows, s_idx, s_free):
            def fetch_indices(first):
                pool.tensor_copy(idx_slots[:, first.slot(2 * RING) // RING, :],
                                 indices[:, bass.ds(first.v * TILES_PER_BATCH,
                                                    RING * TILES_PER_BATCH)]).then_inc(s_idx, 1)

            def gather(b):
                if b.i is None and b.off == 0:
                    fetch_indices(b)
                if b.slot(RING) == 0:
                    pool.wait_ge(s_idx, b.uses(RING) + 1)
                for s in s_free:
                    free(pool, s, b, RING)
                if b.slot(RING) == RING - 1 and b.of_next_group():
                    fetch_indices(b.of_next_group())
                elif b.i is not None:
                    pool.nop(nofuse=True)
                for g in range(TILES_PER_BATCH):
                    col = b.slot(RING) * TILES_PER_BATCH + g
                    half = b.slot(2 * RING) // RING
                    pool.indirect_dma_start(
                        out=rows[:, b.slot(RING), g, 0:width], out_offset=None, in_=table,
                        in_offset=bass.IndirectOffsetOnAxis(
                            ap=idx_slots[:, half, col:col + 1], axis=0))\
                        .then_inc(s_rows[b.slot(RING)], 16)
            return gather

        def end_gathers(pool):
            for s in gather_sems:
                pool.wait_ge(s, 16 * TILES_PER_BATCH * N_BATCHES // RING)
            pool.dma_reset(range(gather_sems[0].num, gather_sems[-1].num + 1))

        def tiles_of(t, b):
            return t[:, bass.ds(b.v * TILES_PER_BATCH, TILES_PER_BATCH)]

        def onehot_stage(dve, to, ring, s_onehot, readers):
            def build(b):
                for s in readers:
                    free(dve, s, b, ring)
                wide = [P, TILES_PER_BATCH, P]
                dve.tensor_tensor(to[:, b.slot(ring), :, :],
                                  iota[:, :].unsqueeze(1).to_broadcast(wide),
                                  tiles_of(dst_rel, b).unsqueeze(2).to_broadcast(wide),
                                  ALU.is_equal).then_inc(s_onehot, 1)
            return build

        def read_base(eng, b):
            return eng.value_load(base[0:1, bass.ds(b.v, 1)], min_val=0, max_val=LAST_BASE)

        def turned_bank(b):
            return banks[b.slot(2)][:, 0:BANK // 2].bitcast(BF16)

        def turn_stage(pe, s_onehot, s_turned, s_copied):
            def turn(b):
                done(pe, s_onehot, b)
                free(pe, s_copied, b, 2)
                for g in range(TILES_PER_BATCH):
                    last = pe.transpose(turned_bank(b)[:, g * P:(g + 1) * P],
                                        onehot_b[:, b.slot(ONEHOT_RING), g, :], ident_b[:, :])
                last.then_inc(s_turned, 1)
            return turn

        def copy_turned_stage(act, s_turned, s_copied, s_looked):
            def copy_turned(b):
                done(act, s_turned, b)
                free(act, s_looked, b, 2)
                act.activation(onehotT[:, b.slot(2), :, :].rearrange("p g e -> p (g e)"),
                               turned_bank(b), ACT.Copy).then_inc(s_copied, 1)
            return copy_turned

        def window_loop(name, sweep, finish=None):
            with Phase(nc, name + "_first") as ph:
                s = ph.sem("set")
                block = ph.open()

                @block.vector
                def _(dve):
                    dve.tensor_copy(dst_rel[:, :], dst_rel0[:, :]).then_inc(s, 1)
                    dve.tensor_copy(base[:, :], base0[:, :]).then_inc(s, 1)
                    dve.wait_ge(s, 2)
            windows = nc.values_load(n_windows[0:1, 0:1], min_val=1, max_val=N_PAD // WINDOW + 1)
            with nc.Fori(0, windows):
                sweep()
                with Phase(nc, name + "_next") as ph:
                    s = ph.sem("set")
                    block = ph.open()

                    @block.vector
                    def _(dve):
                        c = Chain(dve, s)
                        if finish:
                            finish(dve, c)
                        c.do(dve.tensor_single_scalar(dst_rel[:, :], dst_rel[:, :],
                                                      float(-WINDOW), ALU.add))
                        c.do(dve.tensor_scalar(base[:, :], base[:, :], WINDOW, LAST_BASE,
                                               ALU.add, ALU.min))

        def clear(name, *regions):
            with Phase(nc, name) as ph:
                s = ph.sem("set")
                block = ph.open()

                @block.vector
                def _(dve):
                    for r, value in regions:
                        dve.memset(r, value).then_inc(s, 1)
                    dve.wait_ge(s, len(regions))

        def sum_sweep(name, width, edge_rows, weighted):
            def sweep():
                with Phase(nc, name) as ph:
                    s_onehot, s_joined, s_sum, s_added, s_idx = (
                        ph.sem(n) for n in ("onehot", "joined", "summed", "added", "idx"))
                    s_rows = ph.use(gather_sems)
                    s_edge = [ph.sem(f"edge{n}") for n in range(RING)]
                    block = ph.open()
                    ew = TILES_PER_BATCH * D_EDGE

                    @block.gpsimd
                    def _(pool):
                        pipeline(pool, [(0, gather_stage(pool, src_idx, node_rows, D, s_rows, s_idx,
                                                         [s_sum]))])
                        end_gathers(pool)

                    if edge_rows:
                        @block.sync
                        def _(sp):
                            def stream(b):
                                free(sp, s_joined, b, RING)
                                sp.dma_start(edge_in[:, b.slot(RING), 0:ew],
                                             a["ea_l"][:, bass.ds(b.v * ew, ew)])\
                                  .then_inc(s_edge[b.slot(RING)], 16)
                            pipeline(sp, [(0, stream)])

                        @block.scalar
                        def _(act):
                            def join(b):
                                landed(act, s_edge, b, 16)
                                free(act, s_sum, b, RING)
                                act.activation(
                                    rows[:, b.slot(RING), :, D:D + D_EDGE],
                                    edge_in[:, b.slot(RING), 0:ew].rearrange(
                                        "p (g f) -> p g f", f=D_EDGE), ACT.Copy)\
                                    .then_inc(s_joined, 1)
                            pipeline(act, [(0, join)])

                    @block.tensor
                    def _(pe):
                        def sums(b):
                            done(pe, s_onehot, b)
                            landed(pe, s_rows, b, 16 * TILES_PER_BATCH)
                            if edge_rows:
                                done(pe, s_joined, b)
                            free(pe, s_added, b, 2)
                            for g in range(TILES_PER_BATCH):
                                last = pe.matmul(banks[b.slot(2)][0:width, 0:P],
                                                 rows[:, b.slot(RING), g, 0:width],
                                                 onehot[:, b.slot(RING), g, :],
                                                 start=(g == 0), stop=(g == TILES_PER_BATCH - 1))
                            last.then_inc(s_sum, 1)
                        pipeline(pe, [(0, sums)])

                    @block.vector
                    def _(dve):
                        def weighted_onehot(b):
                            free(dve, s_sum, b, RING)
                            for g in range(TILES_PER_BATCH):
                                col = bass.ds(b.v * TILES_PER_BATCH + g, 1)
                                last = dve.tensor_scalar(onehot[:, b.slot(RING), g, :], iota[:, :],
                                                         dst_rel[:, col], weight[:, col],
                                                         ALU.is_equal, ALU.mult)
                            last.then_inc(s_onehot, 1)

                        def add(b):
                            done(dve, s_sum, b)
                            at = accT[0:width, bass.ds(read_base(dve, b), WINDOW)]
                            if not b.early(1):
                                dve.wait_ge(s_added, b.v)
                            dve.tensor_tensor(at, banks[b.slot(2)][0:width, 0:P], at, ALU.add)\
                               .then_inc(s_added, 1)
                        build = (weighted_onehot if weighted else
                                 onehot_stage(dve, onehot, RING, s_onehot, [s_sum]))
                        pipeline(dve, [(0, build), (2, add)])
            window_loop(name, sweep)

        def score_sweep(name, layer):
            width = D if layer == 1 else 2 * D

            def sweep():
                with Phase(nc, name) as ph:
                    (s_onehot, s_turned, s_copied, s_penalty, s_looked, s_pre, s_act, s_score,
                     s_masked, s_mturned, s_max, s_row, s_rowmax, s_idx, s_packed, s_kept) = (
                         ph.sem(n) for n in (
                             "onehot", "turned", "copied", "penalty", "looked", "pre", "act",
                             "score", "masked", "mturned", "max", "row", "rowmax", "idx",
                             "packed", "kept"))
                    s_rows = ph.use(gather_sems)
                    s_dma = [ph.sem(f"edge{n}") for n in range(RING)]
                    block = ph.open()
                    indices, table = (src_idx, node_rows) if layer == 1 else (rel_idx, rel_rows)
                    s_read = [s_pre] if layer == 1 else [s_score, s_packed]

                    @block.gpsimd
                    def _(pool):
                        pipeline(pool, [(0, gather_stage(pool, indices, table, width, s_rows,
                                                         s_idx, s_read))])
                        end_gathers(pool)

                    @block.sync
                    def _(sp):
                        def stream(b):
                            free(sp, s_looked, b, RING)
                            sp.dma_start(edge_in[0:D_EDGE, b.slot(RING), :],
                                         a["eaT_l"][:, bass.ds(b.v * BATCH, BATCH)])\
                              .then_inc(s_dma[b.slot(RING)], 16)

                        def store(b):
                            done(sp, s_packed, b)
                            sp.dma_start(spill[bass.ds(b.v, 1), :, :].rearrange("o p f -> (o p) f"),
                                         spill_out[:, b.slot(RING), :])\
                              .then_inc(s_dma[b.slot(RING)], 16)
                        pipeline(sp, [(0, stream if layer == 1 else store)])
                        if layer == 3:
                            for s in s_dma:
                                sp.wait_ge(s, 16 * N_BATCHES // RING)

                    @block.scalar
                    def _(act):
                        def penalties(b):
                            done(act, s_onehot, b)
                            if not b.early(2):
                                act.wait_ge(s_masked, b.v - 1)
                            act.activation(penalty[:, b.slot(2), :, :],
                                           onehot_b[:, b.slot(ONEHOT_RING), :, :], ACT.Copy,
                                           bias=FAR_BELOW, scale=-FAR_BELOW).then_inc(s_penalty, 1)

                        def mask(b):
                            done(act, s_score, b)
                            done(act, s_penalty, b)
                            free(act, s_mturned, b, 2)
                            for g in range(TILES_PER_BATCH):
                                last = act.activation(
                                    masked[:, b.slot(2), g, :], penalty[:, b.slot(2), g, :],
                                    ACT.Identity, bias=fresh_slots[:, b.slot(2 * RING), g:g + 1])
                            last.then_inc(s_masked, 1)

                        def pack(b):
                            landed(act, s_rows, b, 16 * TILES_PER_BATCH)
                            if not b.early(RING):
                                act.wait_ge(s_dma[b.slot(RING)], b.uses(RING) * 16)
                            act.activation(
                                spill_out[:, b.slot(RING), :].rearrange("p (g f) -> p g f", f=D),
                                rows[:, b.slot(RING), :, 0:D], ACT.Copy).then_inc(s_packed, 1)
                        stages = [(4, mask),
                                  (1, copy_turned_stage(act, s_turned, s_copied, s_looked)),
                                  (2, penalties)]
                        if layer == 3:
                            stages.append((3, pack))
                        pipeline(act, stages)

                    @block.tensor
                    def _(pe):
                        def look(b):
                            done(pe, s_copied, b)
                            free(pe, s_pre if layer == 1 else s_score, b, 2)
                            if layer == 1:
                                landed(pe, s_dma, b, 16)
                            at = read_base(pe, b) * (D // WINDOW_STEP)
                            parts = [by_chunk[:, :].bitcast(BF16)[:, bass.ds(at * 2, D)],
                                     by_chunk[:, :].bitcast(BF16)[:, bass.ds(at * 2 + D, D)],
                                     table_2[:, bass.ds(at, D)]]
                            for g in range(TILES_PER_BATCH):
                                to = banks[2 + b.slot(2)][:, g * D:(g + 1) * D]
                                for n, part in enumerate(parts):
                                    last = pe.matmul(to, onehotT[:, b.slot(2), g, :], part,
                                                     start=(n == 0),
                                                     stop=(layer == 3 and n == PARTS - 1))
                                if layer == 1:
                                    last = pe.matmul(to, edge_in[0:D_EDGE, b.slot(RING),
                                                                 g * P:(g + 1) * P],
                                                     w1_e[:, :], start=False, stop=True)
                            last.then_inc(s_looked, 1)

                        def turn_masked(b):
                            done(pe, s_masked, b)
                            free(pe, s_max, b, 2)
                            for g in range(TILES_PER_BATCH):
                                last = pe.transpose(banks[4 + b.slot(2)][:, g * P:(g + 1) * P],
                                                    masked[:, b.slot(2), g, :], ident[:, :])
                            last.then_inc(s_mturned, 1)

                        def turn_max(b):
                            done(pe, s_max, b)
                            free(pe, s_rowmax, b, 2)
                            pe.matmul(banks[6 + b.slot(2)][96:97, 0:P],
                                      batch_max[:, b.slot(2):b.slot(2) + 1], ident[:, :],
                                      start=True, stop=True).then_inc(s_row, 1)
                        pipeline(pe, [(1, turn_stage(pe, s_onehot, s_turned, s_copied)), (2, look),
                                      (5, turn_masked), (7, turn_max)])

                    @block.vector
                    def _(dve):
                        def keep(first, slot):
                            dve.tensor_copy(
                                fresh[:, bass.ds(first * TILES_PER_BATCH, RING * TILES_PER_BATCH)],
                                fresh_slots[:, slot:slot + RING, :].rearrange("p s g -> p (s g)"))\
                               .then_inc(s_kept, 1)

                        def scores(b):
                            s2 = b.slot(2)
                            looked = banks[2 + s2][:, 0:TILES_PER_BATCH * D].rearrange(
                                "p (g f) -> p g f", f=D)
                            done(dve, s_looked, b)
                            landed(dve, s_rows, b, 16 * TILES_PER_BATCH)
                            if layer == 1:
                                dve.tensor_tensor(pre[:, s2, :, :], looked,
                                                  rows[:, b.slot(RING), :, 0:D], ALU.add)\
                                   .then_inc(s_pre, 1)
                                done(dve, s_pre, b)
                                dve.scalar_tensor_tensor(pre[:, s2, :, :], pre[:, s2, :, :], SLOPE,
                                                         pre[:, s2, :, :], ALU.mult, ALU.max)\
                                   .then_inc(s_act, 1)
                                done(dve, s_act, b)
                            if not b.early(1):
                                dve.wait_ge(s_score, b.v)
                            if b.slot(RING) == 0 and not b.early(RING):
                                keep(b.v - RING, (b.off - RING) % (2 * RING))
                                dve.wait_ge(s_kept, b.uses(RING))
                            for g in range(TILES_PER_BATCH):
                                left, right = (
                                    (pre[:, s2, g, :], a_w[:, :]) if layer == 1 else
                                    (looked[:, g, :], rows[:, b.slot(RING), g, D:2 * D]))
                                last = dve.tensor_tensor_reduce(
                                    out=products_out[:, g, :], in0=left, in1=right, scale=1.0,
                                    scalar=0.0, op0=ALU.mult, op1=ALU.add,
                                    accum_out=fresh_slots[:, b.slot(2 * RING), g:g + 1])
                            last.then_inc(s_score, 1)

                        def maxima(b):
                            done(dve, s_mturned, b)
                            free(dve, s_row, b, 2)
                            dve.reduce_max(batch_max[:, b.slot(2):b.slot(2) + 1],
                                           banks[4 + b.slot(2)][:, :], AX).then_inc(s_max, 1)

                        def keep_max(b):
                            done(dve, s_row, b)
                            at = max_row[:, bass.ds(read_base(dve, b), WINDOW)]
                            if not b.early(1):
                                dve.wait_ge(s_rowmax, b.v)
                            dve.tensor_tensor(at, banks[6 + b.slot(2)][96:97, 0:P], at, ALU.max)\
                               .then_inc(s_rowmax, 1)
                        readers = [s_turned, s_penalty]
                        pipeline(dve, [(8, keep_max), (6, maxima),
                                       (0, onehot_stage(dve, onehot_b, ONEHOT_RING, s_onehot,
                                                        readers)), (3, scores)])
                        dve.wait_ge(s_score, N_BATCHES)
                        keep(N_BATCHES - RING, (N_BATCHES - RING) % (2 * RING))

            def finish(dve, c):
                by, op = (a_b[:, 0:1], ALU.add) if layer == 1 else (ATT_SCALE, ALU.mult)
                c.do(dve.tensor_scalar(fresh[:, :], fresh[:, :], by, None, op))
                c.do(dve.scalar_tensor_tensor(fresh[:, :], dst_rel[:, :], 0.0, fresh[:, :],
                                              ALU.is_ge, ALU.mult))
                c.do(dve.scalar_tensor_tensor(fresh[:, :], dst_rel[:, :], float(WINDOW),
                                              fresh[:, :], ALU.is_lt, ALU.mult))
                c.do(dve.tensor_tensor(score[:, :], score[:, :], fresh[:, :], ALU.add))
            window_loop(name, sweep, finish)
            with Phase(nc, name + "_max") as ph:
                s = ph.sem("set")
                block = ph.open()

                @block.vector
                def _(dve):
                    by, op = (a_b[96:97, 0:1], ALU.add) if layer == 1 else (ATT_SCALE, ALU.mult)
                    dve.tensor_scalar(max_row, max_row, by, None, op).then_inc(s, 1)
                    dve.wait_ge(s, 1)

        def softmax_sweep(name, n_heads, messages):
            nv = TILES_PER_BATCH * n_heads
            n_sums = n_heads if messages else PARTS

            def sweep():
                with Phase(nc, name) as ph:
                    (s_onehot, s_turned, s_copied, s_looked, s_joined, s_diff, s_clamped, s_exp,
                     s_wa, s_wb, s_sum, s_added, s_wide, s_chain, s_parts) = (
                         ph.sem(n) for n in (
                             "onehot", "turned", "copied", "looked", "joined", "diff", "clamped",
                             "exp", "weighted_a", "weighted_b", "summed", "added", "wide",
                             "chain", "parts"))
                    onehot_f = rows[:, :, :, :]
                    s_msg = [ph.sem(f"msg{n}") for n in range(RING)]
                    block = ph.open()
                    exv = ex[:, :, 0:nv].rearrange("p s (g h) -> p s g h", h=n_heads)
                    weighted = [penalty, masked]
                    sums = [accT, by_chunk]

                    if messages:
                        @block.sync
                        def _(sp):
                            def load(b):
                                free(sp, s_wa, b, RING)
                                free(sp, s_wb, b, RING)
                                sp.dma_start(edge_in[:, b.slot(RING), 0:TILES_PER_BATCH * D],
                                             spill[bass.ds(b.v, 1), :, :].rearrange(
                                                 "o p f -> (o p) f"))\
                                  .then_inc(s_msg[b.slot(RING)], 16)
                            pipeline(sp, [(0, load)])

                    def weigh_stage(eng, which, s_done):
                        def weigh(b):
                            done(eng, s_exp, b)
                            landed(eng, s_msg, b, 16)
                            free(eng, s_sum, b, 2)
                            msg = edge_in[:, b.slot(RING), 0:TILES_PER_BATCH * D].rearrange(
                                "p (g f) -> p g f", f=D)
                            for h in range(2):
                                head = 2 * which + h
                                to = weighted[which][:, b.slot(2), :, h * D:(h + 1) * D]
                                last = eng.tensor_tensor(
                                    to, msg, exv[:, b.slot(RING), :, head:head + 1].to_broadcast(
                                        [P, TILES_PER_BATCH, D]), ALU.mult)
                            last.then_inc(s_done, 1)
                        return weigh

                    if messages:
                        @block.gpsimd
                        def _(pool):
                            pipeline(pool, [(0, weigh_stage(pool, 1, s_wb))])

                    @block.scalar
                    def _(act):
                        def exps(b):
                            done(act, s_clamped, b)
                            free(act, s_sum, b, RING)
                            act.activation(ex[:, b.slot(RING), 0:nv], ex_in[:, b.slot(2), 0:nv],
                                           ACT.Exp).then_inc(s_exp, 1)

                        def widen(b):
                            done(act, s_onehot, b)
                            free(act, s_sum, b, RING)
                            act.activation(onehot_f[:, b.slot(RING), :, :],
                                           onehot_b[:, b.slot(ONEHOT_RING), :, :], ACT.Copy)\
                               .then_inc(s_wide, 1)
                        pipeline(act, [(1, copy_turned_stage(act, s_turned, s_copied, s_looked)),
                                       (4, exps)] + ([(5, widen)] if messages else []))

                    @block.tensor
                    def _(pe):
                        def look(b):
                            done(pe, s_copied, b)
                            free(pe, s_joined, b, 2)
                            at = (read_base(pe, b) // WINDOW_STEP) * (PARTS * n_heads)
                            w = PARTS * n_heads
                            for g in range(TILES_PER_BATCH):
                                last = pe.matmul(
                                    banks[2 + b.slot(2)][:, g * w:(g + 1) * w],
                                    onehotT[:, b.slot(2), g, :],
                                    small_by_chunk[:, bass.ds(at, w)], start=True, stop=True)
                            last.then_inc(s_looked, 1)

                        def sum_up(b):
                            done(pe, s_exp, b)
                            if messages:
                                done(pe, s_wa, b)
                                done(pe, s_wb, b)
                                done(pe, s_wide, b)
                            else:
                                done(pe, s_parts, b)
                            free(pe, s_added, b, 1)
                            for which in range(2 if messages else 0):
                                for g in range(TILES_PER_BATCH):
                                    pe.matmul(banks[4 + which][:, 0:P],
                                              weighted[which][:, b.slot(2), g, :],
                                              onehot_f[:, b.slot(RING), g, :], start=(g == 0),
                                              stop=(g == TILES_PER_BATCH - 1))
                            for g in range(TILES_PER_BATCH):
                                marks, weights = (
                                    (onehot_f[:, b.slot(RING), g, :], exv[:, b.slot(RING), g, :])
                                    if messages else
                                    (onehot_b[:, b.slot(ONEHOT_RING), g, :],
                                     ex_parts[:, b.slot(RING), g, :]))
                                last = pe.matmul(banks[6][0:n_sums, 0:P], weights, marks,
                                                 start=(g == 0), stop=(g == TILES_PER_BATCH - 1))
                            last.then_inc(s_sum, 1)
                        pipeline(pe, [(1, turn_stage(pe, s_onehot, s_turned, s_copied)), (2, look),
                                      (6, sum_up)])

                    @block.vector
                    def _(dve):
                        def diffs(b):
                            s2 = b.slot(2)
                            done(dve, s_looked, b)
                            free(dve, s_exp, b, 2)
                            v = ex_in[:, s2, 0:nv]
                            by_tile = v.rearrange("p (g h) -> p g h", h=n_heads)
                            dve.reduce_sum(by_tile, banks[2 + s2][:, 0:nv * PARTS].rearrange(
                                "p (g s h) -> p g h s", s=PARTS, h=n_heads), AX)\
                               .then_inc(s_joined, 1)
                            done(dve, s_joined, b)
                            dve.tensor_tensor(
                                by_tile, by_tile, tiles_of(score, b).unsqueeze(2).to_broadcast(
                                    [P, TILES_PER_BATCH, n_heads]), ALU.add).then_inc(s_diff, 1)
                            done(dve, s_diff, b)
                            dve.tensor_single_scalar(v, v, 0.0, ALU.min).then_inc(s_clamped, 1)

                        def part(b):
                            done(dve, s_exp, b)
                            free(dve, s_sum, b, RING)
                            value, left = ex[:, b.slot(RING), 0:nv], ex_left[:, b.slot(2), :]
                            parts = [ex_parts[:, b.slot(RING), :, n] for n in range(PARTS)]
                            at = b.v * PARTS
                            dve.tensor_copy(parts[0], value).then_inc(s_chain, 1)
                            dve.wait_ge(s_chain, at + 1)
                            dve.tensor_tensor(left, value, parts[0], ALU.subtract)\
                               .then_inc(s_chain, 1)
                            dve.wait_ge(s_chain, at + 2)
                            dve.tensor_copy(parts[1], left).then_inc(s_chain, 1)
                            dve.wait_ge(s_chain, at + 3)
                            dve.tensor_tensor(parts[2], left, parts[1], ALU.subtract)\
                               .then_inc(s_parts, 1)

                        def add(b):
                            done(dve, s_sum, b)
                            at = bass.ds(read_base(dve, b), WINDOW)
                            if not b.early(1):
                                dve.wait_ge(s_added, b.v)
                            for which in range(2 if messages else 0):
                                to = sums[which][:, at]
                                dve.tensor_tensor(to, banks[4 + which][:, 0:P], to, ALU.add)
                            to = featT[0:n_sums, at]
                            dve.tensor_tensor(to, banks[6][0:n_sums, 0:P], to, ALU.add)\
                               .then_inc(s_added, 1)
                        readers = [s_turned, s_wide if messages else s_sum]
                        pipeline(dve, [(7, add),
                                       (0, onehot_stage(dve, onehot_b, ONEHOT_RING, s_onehot,
                                                        readers)),
                                       (3, diffs),
                                       (5, weigh_stage(dve, 0, s_wa) if messages else part)])
            window_loop(name, sweep)

        layer_norm("norm0", rows_out=True)
        clear("clear0", (accT[:, :], 0.0))
        sum_sweep("sum0", D + D_EDGE, True, False)

        def matmuls0(pe, j, bank, place):
            to = bank[:, place * D:(place + 1) * D]
            at = slice(j * P, (j + 1) * P)
            pe.matmul(to, featT[0:D + 1, at], w0_self[:, :], start=True, stop=False)
            return pe.matmul(to, accT[0:D + D_EDGE, at], w0_agg[:, :], start=False, stop=True)

        def take0(eng, c, n, items, bank):
            to = x[:, items[0]:items[-1] + 1, :]
            return eng.scalar_tensor_tensor(
                to, bank[:, 0:len(items) * D].rearrange("p (j d) -> p j d", d=D), 0.0, to,
                ALU.max, ALU.add)
        take0.both = False
        products("out0", NODE_TILES, BANK // D, matmuls0, take0)

        layer_norm("norm1")

        def matmuls1q(pe, j, bank, place):
            return pe.matmul(bank[:, place * D:(place + 1) * D], featT[0:D + 3, j * P:(j + 1) * P],
                             w1_q[:, :], start=True, stop=True)

        def take1q(eng, c, n, items, bank):
            return copy(eng, edge_in[:, n % RING, 0:len(items) * D], bank[:, 0:len(items) * D])

        def store1q(sp, n, items):
            return sp.dma_start(rows_view(items), edge_in[:, n % RING, 0:len(items) * D].rearrange(
                "p (j d) -> p j d", d=D))
        take1q.both = True
        products("table1q", NODE_TILES, BANK // D, matmuls1q, take1q, store1q)
        table_by_chunk("table1k", w1_k, D)
        clear("clear1", (max_row, FAR_BELOW), (score[:, :], 0.0))
        score_sweep("score1", 1)

        def matmuls1m(pe, c, bank, place):
            at = c * WINDOW_STEP
            return pe.matmul(bank[:, place:place + 1], max_row[:, at:at + P], one[96:97, :],
                             start=True, stop=True)

        def take1m(eng, c, n, items, bank):
            value, left = (v.rearrange("p g f -> p (g f)") for v in (pre[:, 0, :, :],
                                                                     pre[:, 1, :, :]))
            value, left = value[:, 0:N_CHUNKS], left[:, 0:N_CHUNKS]
            c.do(eng.tensor_single_scalar(value, bank[:, 0:N_CHUNKS], -1.0, ALU.mult))
            table = small_by_chunk[:, 0:N_CHUNKS * PARTS].rearrange("p (c s) -> p c s", s=PARTS)
            return split(eng, c, value, left, [table[:, :, n] for n in range(PARTS)])
        take1m.both = False
        products("max1", N_CHUNKS, N_CHUNKS, matmuls1m, take1m)

        def matmuls1v(pe, j, bank, place):
            return pe.matmul(bank[:, place * D:(place + 1) * D], featT[0:D + 1, j * P:(j + 1) * P],
                             w1_v[:, :], start=True, stop=True)

        values1 = by_chunk[:, 0:NODE_TILES * D]

        def take1v(eng, c, n, items, bank):
            return copy(eng, values1[:, items[0] * D:(items[-1] + 1) * D], bank[:, 0:len(items) * D])
        take1v.both = True
        products("value1", NODE_TILES, BANK // D, matmuls1v, take1v)
        clear("clear1d", (featT[0:N_ACTIVE, :], 0.0))
        softmax_sweep("soft1", 1, False)

        def matmuls1d(pe, j, bank, place):
            return pe.transpose(bank[:, place * PARTS:(place + 1) * PARTS],
                                featT[0:PARTS, j * P:(j + 1) * P], ident[0:PARTS, 0:PARTS])

        def take1d(eng, c, n, items, bank):
            d = node_b[:, :]
            c.do(eng.reduce_sum(d, bank[:, 0:NODE_TILES * PARTS].rearrange(
                "p (j s) -> p j s", s=PARTS), AX))
            c.do(eng.tensor_single_scalar(node_a[:, :], d, TINY, ALU.max))
            c.do(eng.reciprocal(node_a[:, :], node_a[:, :]))
            c.do(eng.tensor_tensor(node_a[:, :], d, node_a[:, :], ALU.mult))
            v = values1.rearrange("p (j d) -> p j d", d=D)
            c.do(eng.tensor_tensor(v, v, node_a[:, :].unsqueeze(2).to_broadcast([P, NODE_TILES, D]),
                                   ALU.mult))
            return eng.tensor_tensor(x[:, :, :], x[:, :, :], v, ALU.add)
        take1d.both = False
        products("out1", NODE_TILES, NODE_TILES, matmuls1d, take1d)

        layer_norm("norm2", rows_out=True)
        clear("clear2", (accT[:, :], 0.0))
        sum_sweep("sum2", D, False, True)

        def matmuls2(pe, j, bank, place):
            return pe.transpose(bank[:, place * D:(place + 1) * D], accT[0:D, j * P:(j + 1) * P],
                                ident[0:D, 0:D])

        def take2(eng, c, n, items, bank):
            to = x[:, items[0]:items[-1] + 1, :]
            return eng.tensor_tensor(
                to, bank[:, 0:len(items) * D].rearrange("p (j d) -> p j d", d=D), to, ALU.add)
        take2.both = False
        products("out2", NODE_TILES, BANK // D, matmuls2, take2)

        layer_norm("norm3")
        with Phase(nc, "weights3") as ph:
            s_chain, s_rel, s_pe, s_t, s_key, s_copied, s_zero, s_bias = (
                ph.sem(n) for n in ("chain", "rel", "pe", "turned", "key", "copied", "zero",
                                    "bias"))
            block = ph.open()

            @block.sync
            def _(sp):
                sp.wait_ge(s_zero, 1)
                sp.dma_start(w3_table[D + 1:D + 2, :, D:2 * D],
                             a["w3_bk"].rearrange("i (r o) -> i r o", o=D)).then_inc(s_bias, 16)
                sp.wait_ge(s_bias, 16)

            @block.vector
            def _(dve):
                c = Chain(dve, s_chain)
                dve.memset(w3_table[D:D + 2, :, :], 0.0).then_inc(s_zero, 1)
                c.do(dve.reduce_sum(rel_mean[:, :], w3_rel[:, :, :], AX))
                dve.tensor_single_scalar(rel_mean[:, :], rel_mean[:, :], 1.0 / D, ALU.mult)\
                   .then_inc(s_rel, 1)
                dve.tensor_copy(w3_table[0:D, :, 0:D], w3_rel[:, :, :]).then_inc(s_copied, 1)
                for r in range(N_REL):
                    dve.tensor_copy(w3_table[0:D, r, D:2 * D], w3_k[:, 0, :]).then_inc(s_copied, 1)
                dve.wait_ge(s_pe, 1)
                dve.wait_ge(s_zero, 1)
                dve.tensor_copy(w3_table[D:D + 1, :, D:2 * D],
                                banks[0][0:1, :].rearrange("p (r o) -> p r o", o=D))\
                   .then_inc(s_copied, 1)
                dve.wait_ge(s_pe, 2)
                dve.tensor_copy(rulesT[:, :], banks[1][0:D, 0:N_ACTIVE]).then_inc(s_t, 1)
                dve.wait_ge(s_pe, 3)
                dve.tensor_copy(rule_keyT[:, :], banks[2][0:D, 0:N_ACTIVE]).then_inc(s_key, 1)
                dve.wait_ge(s_pe, 4)
                dve.tensor_copy(w3_rule[:, :], banks[3][0:D + 1, 0:N_ACTIVE]).then_inc(s_copied, 1)
                dve.wait_ge(s_copied, 3 + N_REL)

            @block.tensor
            def _(pe):
                pe.wait_ge(s_rel, 1)
                for r in range(N_REL):
                    last = pe.matmul(banks[0][0:1, r * D:(r + 1) * D], rel_mean[:, r:r + 1],
                                     w3_k[:, 1, :], start=True, stop=True)
                last.then_inc(s_pe, 1)
                pe.transpose(banks[1][0:D, 0:N_ACTIVE], rules[:, :],
                             ident[0:N_ACTIVE, 0:N_ACTIVE]).then_inc(s_pe, 1)
                pe.wait_ge(s_t, 1)
                pe.matmul(banks[2][0:D, 0:N_ACTIVE], w3_k[:, 2, :], rulesT[:, :], start=True,
                          stop=True).then_inc(s_pe, 1)
                pe.wait_ge(s_key, 1)
                pe.matmul(banks[3][0:D + 1, 0:N_ACTIVE], w3_qT[:, :], rule_keyT[:, :], start=True,
                          stop=True).then_inc(s_pe, 1)

        half_cols = N_REL * 2 * D // 2
        table_cols = w3_table[:, :, :].rearrange("i r o -> i (r o)")
        rel_rows_v = rel_rows.rearrange("(j p r) o -> j p (r o)", p=P, r=N_REL)

        def matmuls3t(pe, item, bank, place):
            j, half = divmod(item, 2)
            return pe.matmul(bank[:, :], featT[0:D + 2, j * P:(j + 1) * P],
                             table_cols[:, half * half_cols:(half + 1) * half_cols],
                             start=True, stop=True)

        def take3t(eng, c, n, items, bank):
            return copy(eng, edge_in[:, n % RING, :], bank[:, :])

        def store3t(sp, n, items):
            j, half = divmod(items[0], 2)
            return sp.dma_start(rel_rows_v[j, :, half * half_cols:(half + 1) * half_cols],
                                edge_in[:, n % RING, :])
        take3t.both = True
        products("table3", 2 * NODE_TILES, 1, matmuls3t, take3t, store3t)
        table_by_chunk("table3q", w3_q, D + 1)
        clear("clear3", (max_row, FAR_BELOW), (score[:, :], 0.0))
        score_sweep("score3", 3)

        def matmuls3m(pe, c, bank, place):
            at = c * WINDOW_STEP
            w = N_ACTIVE + 1
            pe.matmul(bank[:, place * w:place * w + N_ACTIVE], featT[0:D + 1, at:at + P],
                      w3_rule[:, :], start=True, stop=True)
            return pe.matmul(bank[:, place * w + N_ACTIVE:(place + 1) * w], max_row[:, at:at + P],
                             one[96:97, :], start=True, stop=True)

        def take3m(eng, c, n, items, bank):
            k = len(items)
            v = bank[:, 0:k * (N_ACTIVE + 1)].rearrange("p (c r) -> p c r", r=N_ACTIVE + 1)
            rule_score = pre[:, 0, :, :].rearrange("p g f -> p (g f)")[:, 0:k * N_ACTIVE]\
                .rearrange("p (c r) -> p c r", r=N_ACTIVE)
            base_max = node_b[:, 0:k]
            to, left = (rows[:, s, 0:2, :].rearrange("p g f -> p (g f)")[:, 0:k * N_ACTIVE]
                        .rearrange("p (c r) -> p c r", r=N_ACTIVE) for s in range(2))
            table = small_by_chunk[:, :].rearrange("p (c s r) -> p c s r", s=PARTS, r=N_ACTIVE)
            c.do(eng.tensor_single_scalar(rule_score, v[:, :, 0:N_ACTIVE], ATT_SCALE, ALU.mult))
            c.do(eng.tensor_copy(base_max, v[:, :, N_ACTIVE]))
            c.do(eng.tensor_tensor(to, rule_score,
                                   base_max.unsqueeze(2).to_broadcast([P, k, N_ACTIVE]), ALU.add))
            c.do(eng.tensor_tensor(to, rule_score, to, ALU.subtract))
            return split(eng, c, to, left, [table[:, items[0]:items[-1] + 1, p, :]
                                            for p in range(PARTS)])
        take3m.both = False
        products("max3", N_CHUNKS, 50, matmuls3m, take3m)
        clear("clear3d", (featT[0:N_ACTIVE, :], 0.0), (accT[:, :], 0.0),
              (by_chunk[:, 0:N_PAD], 0.0))
        softmax_sweep("soft3", N_ACTIVE, True)

        def matmuls3d(pe, j, bank, place):
            return pe.transpose(bank[:, place * N_ACTIVE:(place + 1) * N_ACTIVE],
                                featT[0:N_ACTIVE, j * P:(j + 1) * P], ident[0:N_ACTIVE, 0:N_ACTIVE])

        denom = pre[:, :, :, :].rearrange("p s g f -> p (s g f)")[:, 0:NODE_TILES * N_ACTIVE]

        def take3d(eng, c, n, items, bank):
            c.do(eng.tensor_single_scalar(denom, bank[:, 0:NODE_TILES * N_ACTIVE], TINY, ALU.max))
            c.do(eng.reciprocal(denom, denom))
            return eng.tensor_single_scalar(denom, denom, 1.0 / N_ACTIVE, ALU.mult)
        take3d.both = False
        products("denom3", NODE_TILES, NODE_TILES, matmuls3d, take3d)

        def matmuls3o(pe, j, bank, place):
            pe.transpose(bank[:, 0:P], accT[:, j * P:(j + 1) * P], ident[:, :])
            return pe.transpose(bank[:, P:2 * P], by_chunk[:, j * P:(j + 1) * P], ident[:, :])

        message3 = featT[:, 0:NODE_TILES * D].rearrange("p (j d) -> p j d", d=D)

        def take3o(eng, c, n, items, bank):
            j = items[0]
            tmp = rows[:, n % RING, :, 0:D]
            c.do(eng.tensor_tensor(
                tmp, bank[:, 0:2 * P].rearrange("p (h d) -> p h d", d=D),
                denom[:, j * N_ACTIVE:(j + 1) * N_ACTIVE].unsqueeze(2).to_broadcast(
                    [P, N_ACTIVE, D]), ALU.mult))
            return eng.reduce_sum(message3[:, j, :], tmp.rearrange("p h d -> p d h"), AX)
        take3o.both = False
        products("mean3", NODE_TILES, 1, matmuls3o, take3o)

        with Phase(nc, "out3") as ph:
            s_chain, s_var, s_std, s_out, s_x = (
                ph.sem(n) for n in ("chain", "var", "std", "out", "x"))
            block = ph.open()

            @block.vector
            def _(dve):
                c = Chain(dve, s_chain)
                wide = [P, NODE_TILES, D]

                def vec(n):
                    return bias3[:, n:n + 1, :].to_broadcast(wide)
                c.do(dve.tensor_tensor(message3, message3, vec(0), ALU.add))
                c.do(dve.reduce_sum(node_a[:, :], message3, AX))
                c.do(dve.tensor_single_scalar(node_a[:, :], node_a[:, :], 1.0 / D, ALU.mult))
                c.do(dve.tensor_tensor(message3, message3,
                                       node_a[:, :].unsqueeze(2).to_broadcast(wide), ALU.subtract))
                c.do(dve.tensor_tensor(centred, message3, message3, ALU.mult))
                c.do(dve.reduce_sum(node_a[:, :], centred, AX))
                dve.tensor_scalar(node_a[:, :], node_a[:, :], 1.0 / D, LN_EPS, ALU.mult, ALU.add)\
                   .then_inc(s_var, 1)
                dve.wait_ge(s_std, 1)
                c.do(dve.reciprocal(node_b[:, :], node_b[:, :]))
                c.do(dve.tensor_tensor(message3, message3,
                                       node_b[:, :].unsqueeze(2).to_broadcast(wide), ALU.mult))
                c.do(dve.tensor_tensor(message3, message3, vec(1), ALU.mult))
                c.do(dve.tensor_tensor(message3, message3, vec(2), ALU.add))
                dve.scalar_tensor_tensor(x[:, :, :], message3, 0.0, x[:, :, :], ALU.max, ALU.add)\
                   .then_inc(s_x, 1)

            @block.scalar
            def _(act):
                act.wait_ge(s_var, 1)
                act.activation(node_b[:, :], node_a[:, :], ACT.Sqrt).then_inc(s_std, 1)

            @block.sync
            def _(sp):
                sp.wait_ge(s_x, 1)
                sp.dma_start(out, x[:, :, :].rearrange("p j d -> p (j d)")).then_inc(s_out, 16)
                sp.wait_ge(s_out, 16)


def kernel(**inputs):
    import concourse.bacc as bacc
    from concourse.bass_utils import run_bass_kernel_spmd

    def arr(name):
        return np.asarray(inputs[name])

    def edge_major(v, fill):
        return np.pad(v, (0, E_PAD - N_EDGES), constant_values=fill).reshape(N_TILES, P).T

    def row(v):
        return v.reshape(1, -1)

    dst = np.pad(arr("dst"), (0, E_PAD - N_EDGES), constant_values=N_NODES)
    ea = np.pad(arr("edge_attr_32"), ((0, E_PAD - N_EDGES), (0, 0)))
    w0 = arr("L0_gnn_W").T
    wq3, bq3 = arr("L3_gnn_Wq_w"), row(arr("L3_gnn_Wq_bias"))
    arrays = {
        "x_l": np.pad(arr("x"), ((0, N_PAD - N_NODES), (0, 0))).reshape(NODE_TILES, P, D)
        .transpose(1, 0, 2).reshape(P, NODE_TILES * D),
        "src_l": edge_major(arr("src"), 0),
        "dst_l": dst.reshape(N_TILES, P).T,
        "dst_b": dst.reshape(BATCH_ROWS, 4 * BATCH),
        "type_l": edge_major(arr("edge_type_8"), 0),
        "w_l": edge_major(arr("edge_weight"), 0),
        "w2_l": edge_major(arr("edge_weight_n2"), 0),
        "ea_l": ea.reshape(N_TILES, P, D_EDGE).transpose(1, 0, 2).reshape(P, N_TILES * D_EDGE),
        "eaT_l": ea.T,
        "w0_self": np.concatenate([w0[0:D], row(arr("L0_gnn_b"))]),
        "w0_agg": w0[D:],
        "w1_q": np.concatenate([arr("L1_gnn_W_q"), row(arr("L1_gnn_b_q")), row(arr("L1_gnn_b_k")),
                                row(arr("L1_gnn_b_e"))]),
        "w1_k": arr("L1_gnn_W_k"),
        "w1_v": np.concatenate([arr("L1_gnn_W_v"), row(arr("L1_gnn_b_v"))]),
        "w1_e": arr("L1_gnn_W_e"),
        "a_w": row(arr("L1_gnn_a_w")),
        "a_b": row(arr("L1_gnn_a_b")),
        "w3_rel": arr("L3_gnn_W_r").transpose(1, 0, 2).reshape(D, N_REL * D),
        "w3_q": np.concatenate([wq3, bq3]),
        "w3_qT": np.concatenate([wq3, bq3]).T,
        "w3_k": arr("L3_gnn_Wk_w").reshape(3, D, D).transpose(1, 0, 2).reshape(D, 3 * D),
        "w3_bk": np.tile(row(arr("L3_gnn_Wk_bias")), (1, N_REL)),
        "rule_ids": arr("L3_gnn_rule_ids").reshape(N_ACTIVE, 1),
        "rule_emb": arr("L3_gnn_rule_emb"),
        "bias3": np.concatenate([row(arr("L3_gnn_bias")), row(arr("L3_gnn_ln_g")),
                                 row(arr("L3_gnn_ln_b"))], axis=1),
    }
    arrays = {k: np.ascontiguousarray(v) for k, v in arrays.items()}
    nc = bacc.Bacc("TRN2", target_bir_lowering=False, num_devices=1)
    aps = {k: nc.dram_tensor("in_" + k, v.shape, mybir.dt.from_np(v.dtype), kind="ExternalInput").ap()
           for k, v in arrays.items()}
    out = nc.dram_tensor("out", (P, NODE_TILES * D), F32, kind="ExternalOutput").ap()
    graph_layers(nc, aps, out)
    r = run_bass_kernel_spmd(nc, [{"in_" + k: v for k, v in arrays.items()}], core_ids=[0])
    got = np.asarray(r.results[0]["out"])
    return got.reshape(P, NODE_TILES, D).transpose(1, 0, 2).reshape(N_PAD, D)[:N_NODES]
```
